# Optimizing a Trainium2 kernel written in Bass

```python
import numpy as np
import jax
import jax.numpy as jnp

def _softmax(x, axis=-1):
    return jax.nn.softmax(x, axis=axis)
def _gelu(x):
    return jax.nn.gelu(x, approximate=True)
def _silu(x):
    return jax.nn.silu(x)
def _sigmoid(x):
    return jax.nn.sigmoid(x)
def _layernorm(x, axis=-1, eps=1e-5):
    m = jnp.mean(x, axis=axis, keepdims=True)
    v = jnp.var(x, axis=axis, keepdims=True)
    return (x - m) / jnp.sqrt(v + eps)
def _scatter_add(tgt, idx, src, axis=0):
    return tgt.at[idx].add(src)
def _segment_sum(src, seg, n):
    return jax.ops.segment_sum(src, seg, n)

kernel_name = 'mk_conv_preact_d2_conv_nchw256_7bfb95'

def setup_inputs(seed: int = 0):
    np.random.seed(seed)
    _w = jnp.asarray
    def _rec_inputs():
        import jax
        import jax.numpy as jnp
        _gk = jax.random.key(seed)
        x = -0.0002928 + 1 * jax.random.normal(jax.random.fold_in(_gk, 1), (4, 256, 64, 64), jnp.float32)
        return x
    x = _rec_inputs()
    def _L0_conv_setup():
        import jax, jax.numpy as jnp
        import numpy as np
        DIM = 256
        HEADS = 4
        DIM_HEAD = 32
        HIDDEN = HEADS * DIM_HEAD
        SCALE = DIM_HEAD ** (-0.5)
        EPS = 1e-05
        key = jax.random.key(seed)
        ks = jax.random.split(key, 6)
        b, h, w = (4, 64, 64)
        x = jax.random.normal(ks[0], (b, DIM, h, w), dtype=jnp.float32)
        gamma = jnp.ones((DIM,), dtype=jnp.float32)
        beta = jnp.zeros((DIM,), dtype=jnp.float32)
        w_qkv = jax.random.normal(ks[1], (3 * HIDDEN, DIM), dtype=jnp.float32) * DIM ** (-0.5)
        w_out = jax.random.normal(ks[2], (DIM, HIDDEN), dtype=jnp.float32) * HIDDEN ** (-0.5)
        b_out = jax.random.normal(ks[3], (DIM,), dtype=jnp.float32) * 0.02
        return {'x': x, 'gamma': gamma, 'beta': beta, 'w_qkv': w_qkv, 'w_out': w_out, 'b_out': b_out}
    _L0_conv_all = _L0_conv_setup()
    _L0_conv_in = {k: v for k, v in _L0_conv_all.items() if k in ('gamma', 'beta', 'w_qkv', 'w_out', 'b_out', )}
    del _L0_conv_all

    def _L1_conv_setup():
        import jax, jax.numpy as jnp
        import numpy as np
        K = 3
        PAD = 1
        GROUPS = 32
        EPS = 1e-05

        def _conv2d(x, w, b, pad):
            y = jax.lax.conv_general_dilated(x, w, window_strides=(1, 1), padding=[(pad, pad), (pad, pad)], dimension_numbers=('NCHW', 'OIHW', 'NCHW'))
            return y + b[None, :, None, None]

        def _deform_sample(x, w_off, b_off):
            B, C, H, W = x.shape
            off = _conv2d(x, w_off, b_off, PAD)
            off = off.reshape(B, 2, K * K, H, W)
            dy, dx = (off[:, 0], off[:, 1])
            ky = jnp.repeat(jnp.arange(K, dtype=x.dtype), K)
            kx = jnp.tile(jnp.arange(K, dtype=x.dtype), K)
            hh = jnp.arange(H, dtype=x.dtype)
            ww = jnp.arange(W, dtype=x.dtype)
            py = dy + ky[None, :, None, None] + hh[None, None, :, None]
            px = dx + kx[None, :, None, None] + ww[None, None, None, :]
            Hp, Wp = (H + 2 * PAD, W + 2 * PAD)
            py = jnp.clip(py, 0.0, Hp - 1.0)
            px = jnp.clip(px, 0.0, Wp - 1.0)
            y0 = jnp.floor(py)
            x0 = jnp.floor(px)
            y1 = jnp.minimum(y0 + 1.0, Hp - 1.0)
            x1 = jnp.minimum(x0 + 1.0, Wp - 1.0)
            wy = py - y0
            wx = px - x0
            xp = jnp.pad(x, ((0, 0), (0, 0), (PAD, PAD), (PAD, PAD)))
            xf = xp.reshape(B, C, Hp * Wp)

            def gather(yi, xi):
                idx = (yi.astype(jnp.int32) * Wp + xi.astype(jnp.int32)).reshape(B, -1)
                g = jax.vmap(lambda m, i: m[:, i])(xf, idx)
                return g.reshape(B, C, K * K, H, W)
            w00 = ((1 - wy) * (1 - wx))[:, None]
            w01 = ((1 - wy) * wx)[:, None]
            w10 = (wy * (1 - wx))[:, None]
            w11 = (wy * wx)[:, None]
            v = gather(y0, x0) * w00 + gather(y0, x1) * w01 + gather(y1, x0) * w10 + gather(y1, x1) * w11
            return v

        def _group_norm(y, gn_w, gn_b):
            B, O, H, W = y.shape
            yg = y.reshape(B, GROUPS, O // GROUPS * H * W)
            mu = jnp.mean(yg, axis=2, keepdims=True)
            var = jnp.mean(jnp.square(yg - mu), axis=2, keepdims=True)
            yn = ((yg - mu) * jax.lax.rsqrt(var + EPS)).reshape(B, O, H, W)
            return yn * gn_w[None, :, None, None] + gn_b[None, :, None, None]
        key = jax.random.key(seed)
        ks = jax.random.split(key, 5)
        B, C, O, H, W = (2, 256, 256, 128, 128)
        x = jax.random.normal(ks[0], (B, C, H, W), jnp.float32)
        w_off = jax.random.normal(ks[1], (2 * K * K, C, 3, 3), jnp.float32) * 0.01
        b_off = jnp.zeros((2 * K * K,), jnp.float32)
        w = jax.random.normal(ks[2], (O, C, K, K), jnp.float32) / np.sqrt(C * K * K)
        b = jax.random.normal(ks[3], (O,), jnp.float32) * 0.01
        gn_w = jnp.ones((O,), jnp.float32)
        gn_b = jnp.zeros((O,), jnp.float32)
        return {'x': x, 'w_off': w_off, 'b_off': b_off, 'w': w, 'b': b, 'gn_w': gn_w, 'gn_b': gn_b}
    _L1_conv_all = _L1_conv_setup()
    _L1_conv_in = {k: v for k, v in _L1_conv_all.items() if k in ('w_off', 'b_off', 'w', 'b', 'gn_w', 'gn_b', )}
    del _L1_conv_all

    return {
        "x": x,
        "L0_conv_gamma": _L0_conv_in["gamma"],
        "L0_conv_beta": _L0_conv_in["beta"],
        "L0_conv_w_qkv": _L0_conv_in["w_qkv"],
        "L0_conv_w_out": _L0_conv_in["w_out"],
        "L0_conv_b_out": _L0_conv_in["b_out"],
        "L1_conv_w_off": _L1_conv_in["w_off"],
        "L1_conv_b_off": _L1_conv_in["b_off"],
        "L1_conv_w": _L1_conv_in["w"],
        "L1_conv_b": _L1_conv_in["b"],
        "L1_conv_gn_w": _L1_conv_in["gn_w"],
        "L1_conv_gn_b": _L1_conv_in["gn_b"],
    }

def reference(x, L0_conv_gamma, L0_conv_beta, L0_conv_w_qkv, L0_conv_w_out, L0_conv_b_out, L1_conv_w_off, L1_conv_b_off, L1_conv_w, L1_conv_b, L1_conv_gn_w, L1_conv_gn_b):
    import jax
    import jax.numpy as jnp
    def _L0_conv_ref(x, gamma, beta, w_qkv, w_out, b_out):
        import jax, jax.numpy as jnp
        import numpy as np
        DIM = 256
        HEADS = 4
        DIM_HEAD = 32
        HIDDEN = HEADS * DIM_HEAD
        SCALE = DIM_HEAD ** (-0.5)
        EPS = 1e-05
        b, c, h, w = x.shape
        n = h * w
        mu = jnp.mean(x, axis=(1, 2, 3), keepdims=True)
        var = jnp.var(x, axis=(1, 2, 3), keepdims=True)
        xn = (x - mu) * jax.lax.rsqrt(var + EPS)
        xn = xn * gamma[None, :, None, None] + beta[None, :, None, None]
        qkv = jnp.einsum('bchw,oc->bohw', xn, w_qkv)
        qkv = qkv.reshape(b, 3, HEADS, DIM_HEAD, n)
        q, k, v = (qkv[:, 0], qkv[:, 1], qkv[:, 2])
        q = q * SCALE
        sim = jnp.einsum('bhci,bhcj->bhij', q, k)
        attn = jax.nn.softmax(sim, axis=-1)
        out = jnp.einsum('bhij,bhcj->bhic', attn, v)
        out = out.transpose(0, 1, 3, 2).reshape(b, HIDDEN, h, w)
        y = jnp.einsum('bchw,oc->bohw', out, w_out) + b_out[None, :, None, None]
        return y

    def _L1_conv_ref(x, w_off, b_off, w, b, gn_w, gn_b):
        import jax, jax.numpy as jnp
        import numpy as np
        K = 3
        PAD = 1
        GROUPS = 32
        EPS = 1e-05

        def _conv2d(x, w, b, pad):
            y = jax.lax.conv_general_dilated(x, w, window_strides=(1, 1), padding=[(pad, pad), (pad, pad)], dimension_numbers=('NCHW', 'OIHW', 'NCHW'))
            return y + b[None, :, None, None]

        def _deform_sample(x, w_off, b_off):
            B, C, H, W = x.shape
            off = _conv2d(x, w_off, b_off, PAD)
            off = off.reshape(B, 2, K * K, H, W)
            dy, dx = (off[:, 0], off[:, 1])
            ky = jnp.repeat(jnp.arange(K, dtype=x.dtype), K)
            kx = jnp.tile(jnp.arange(K, dtype=x.dtype), K)
            hh = jnp.arange(H, dtype=x.dtype)
            ww = jnp.arange(W, dtype=x.dtype)
            py = dy + ky[None, :, None, None] + hh[None, None, :, None]
            px = dx + kx[None, :, None, None] + ww[None, None, None, :]
            Hp, Wp = (H + 2 * PAD, W + 2 * PAD)
            py = jnp.clip(py, 0.0, Hp - 1.0)
            px = jnp.clip(px, 0.0, Wp - 1.0)
            y0 = jnp.floor(py)
            x0 = jnp.floor(px)
            y1 = jnp.minimum(y0 + 1.0, Hp - 1.0)
            x1 = jnp.minimum(x0 + 1.0, Wp - 1.0)
            wy = py - y0
            wx = px - x0
            xp = jnp.pad(x, ((0, 0), (0, 0), (PAD, PAD), (PAD, PAD)))
            xf = xp.reshape(B, C, Hp * Wp)

            def gather(yi, xi):
                idx = (yi.astype(jnp.int32) * Wp + xi.astype(jnp.int32)).reshape(B, -1)
                g = jax.vmap(lambda m, i: m[:, i])(xf, idx)
                return g.reshape(B, C, K * K, H, W)
            w00 = ((1 - wy) * (1 - wx))[:, None]
            w01 = ((1 - wy) * wx)[:, None]
            w10 = (wy * (1 - wx))[:, None]
            w11 = (wy * wx)[:, None]
            v = gather(y0, x0) * w00 + gather(y0, x1) * w01 + gather(y1, x0) * w10 + gather(y1, x1) * w11
            return v

        def _group_norm(y, gn_w, gn_b):
            B, O, H, W = y.shape
            yg = y.reshape(B, GROUPS, O // GROUPS * H * W)
            mu = jnp.mean(yg, axis=2, keepdims=True)
            var = jnp.mean(jnp.square(yg - mu), axis=2, keepdims=True)
            yn = ((yg - mu) * jax.lax.rsqrt(var + EPS)).reshape(B, O, H, W)
            return yn * gn_w[None, :, None, None] + gn_b[None, :, None, None]
        v = _deform_sample(x, w_off, b_off)
        O = w.shape[0]
        y = jnp.einsum('bckhw,ock->bohw', v, w.reshape(O, w.shape[1], K * K))
        y = y + b[None, :, None, None]
        return _group_norm(y, gn_w, gn_b)

    def _gn(v, G=32, eps=1e-5):
        B_, C_, H_, W_ = v.shape
        g = v.reshape(B_, G, C_ // G, H_, W_)
        m = jnp.mean(g, axis=(2, 3, 4), keepdims=True)
        s = jnp.var(g, axis=(2, 3, 4), keepdims=True)
        return ((g - m) / jnp.sqrt(s + eps)).reshape(v.shape)

    def _ln_c(v, eps=1e-6):
        m = jnp.mean(v, axis=1, keepdims=True)
        s = jnp.var(v, axis=1, keepdims=True)
        return (v - m) / jnp.sqrt(s + eps)

    def _ln_t(v, eps=1e-5):
        m = jnp.mean(v, axis=-1, keepdims=True)
        s = jnp.var(v, axis=-1, keepdims=True)
        return (v - m) / jnp.sqrt(s + eps)

    def _to_tokens(v):
        B_, C_, H_, W_ = v.shape
        return v.reshape(B_, C_, H_ * W_).transpose(0, 2, 1)
    def _from_tokens(t, like):
        B_, C_, H_, W_ = like.shape
        return t.transpose(0, 2, 1).reshape(B_, C_, H_, W_)

    x = x + _L0_conv_ref(_gn(x), L0_conv_gamma, L0_conv_beta, L0_conv_w_qkv, L0_conv_w_out, L0_conv_b_out)
    x = x + _L1_conv_ref(_gn(x), L1_conv_w_off, L1_conv_b_off, L1_conv_w, L1_conv_b, L1_conv_gn_w, L1_conv_gn_b)
    return x


_drawn_inputs = setup_inputs


def setup_inputs(seed=0):
    import zlib

    import numpy as np

    out = dict(_drawn_inputs(seed))
    spreads = {'L0_conv_gamma': (1.0, 0.2),
     'L0_conv_beta': (0.0, 0.1),
     'L1_conv_b_off': (0.0, 0.1),
     'L1_conv_gn_w': (1.0, 0.2),
     'L1_conv_gn_b': (0.0, 0.1)}
    factors = {'L1_conv_b': 6.2}
    for name, (base, spread) in spreads.items():
        noise = np.random.default_rng([zlib.crc32(name.encode()), seed]).standard_normal(out[name].shape)
        drawn = base * np.exp(spread * noise) if base else spread * noise
        out[name] = jnp.asarray(drawn.astype(out[name].dtype))
    for name, factor in factors.items():
        out[name] = (out[name] * factor).astype(out[name].dtype)
    return out
```

```python
import concourse.bass as bass
from concourse import mybir
from contextlib import ExitStack

F32 = mybir.dt.float32
BF16 = mybir.dt.bfloat16
I32 = mybir.dt.int32
U32 = mybir.dt.uint32
ACT = mybir.ActivationFunctionType
ALU = mybir.AluOpType
AX = mybir.AxisListType

B, C, H, W = 4, 256, 64, 64
P = 128
CC = C // P
N = H * W
NC = 512
CHUNKS = N // NC
HEADS, DH = 4, 32
HID = HEADS * DH
SCALE = DH ** -0.5
JT = N // P
K, TAPS = 3, 9
HP, WP = H + 2, W + 2
EPS = 1e-5
GROUP = C // 32
TILES = N // P
LEAD = WP + 1
PTILES = HP * WP // P
PGROUPS = [4] * (PTILES // 4) + [PTILES % 4]
OFFS = 2 * TAPS
CT = NC // P
SUBS = 2
STEPS = SUBS * TAPS
ST = CT // SUBS
MAX_UNITS = CT * HEADS * CHUNKS
MAX_PER_JT = 5
MAX_FROM = 1
NEG_AT = JT - HEADS


def step_of(jt):
    first, last = 2, JT - 2
    at = {first + s * (last - first) // STEPS: s for s in range(STEPS)}
    return at.get(jt)


def build(nc, x, gamma, beta, wqkvT, woutT, bout, woffT, boff, wcT, bconv, gnw, gnb,
          ident_c, gmean_c, all_c, base_c, out):
    xv = x.rearrange("b (cc p) h w -> b p cc (h w)", p=P)
    ov = out.rearrange("b (cc p) h w -> b p cc (h w)", p=P)
    qkp = nc.dram_tensor("qk_parts", (2, 3, HID, N), BF16).ap()
    x1s = nc.dram_tensor("x1_scratch", (B, P, CC, N), F32).ap()
    ys = nc.dram_tensor("y_scratch", (P, CC, N), F32).ap()
    tab = nc.dram_tensor("corner_table", (LEAD + HP * WP, 4 * C), F32).ap()

    ctx = ExitStack()
    with ctx:
        def sb(name, shape, dt=F32):
            return ctx.enter_context(nc.sbuf_tensor(name, shape, dt))

        ident = sb("ident", [P, P])
        identb = sb("identb", [P, P], BF16)
        gmean = sb("gmean", [P, P])
        allmean = sb("allmean", [P, P])
        ones = sb("ones", [P, DH])
        base = sb("base", [P, TILES, OFFS])
        wqkv = sb("wqkv", [P, CC, 3 * HID])
        wout = sb("wout", [P, C])
        woff = sb("woff", [P, CC * TAPS, DH])
        wc = sb("wc", [P, CC * TAPS, C])
        vecs = sb("vecs", [P, 6, CC])
        v_gamma, v_beta, v_bout, v_bconv, v_gnw, v_gnb = (vecs[:, i, :] for i in range(6))
        v_boff = sb("v_boff", [P, 1])

        KBYTES = HP * WP * CC * 2 + CC * N * 2
        kk = sb("kk", [P, KBYTES], BF16)
        kA = kk[:, 0:HEADS * N].rearrange("p (h j) -> p h j", h=HEADS)
        kB = kk[:, HEADS * N:2 * HEADS * N].rearrange("p (h j) -> p h j", h=HEADS)
        h1 = kk[:, 0:HP * WP * CC * 2].bitcast(F32).rearrange("p (cc y x) -> p cc y x", cc=CC, x=WP)
        h1flat = h1.rearrange("p cc y x -> p cc (y x)")
        xs = kk[:, HP * WP * CC * 2:KBYTES].bitcast(F32).rearrange("p (cc n) -> p cc n", cc=CC)

        vsb = sb("vsb", [P, JT, HID])
        qnA = sb("qnA", [P, HEADS, NC], BF16)
        qnB = sb("qnB", [P, HEADS, NC], BF16)
        qcA = sb("qcA", [P, HEADS, NC], BF16)
        qcB = sb("qcB", [P, HEADS, NC], BF16)
        probs = [sb(f"probs{i}", [P, HEADS, NC]) for i in range(2)]
        pflat = [t[:, :, :].rearrange("p h n -> p (h n)") for t in probs]
        parts = [sb(f"parts{i}", [P, 3, NC], BF16) for i in range(2)]
        ptmp = [sb(f"ptmp{i}", [P, NC]) for i in range(2)]
        mx = sb("mx", [P, CT * HEADS, CHUNKS])
        neg = sb("neg", [P, CT * HEADS])
        neg2 = sb("neg2", [P, CT * HEADS])
        negp = sb("negp", [P, CT * HEADS, 3], BF16)
        rsum = sb("rsum", [P, NC])
        an = sb("an", [P, NC])
        xr = sb("xr", [P, CC, NC])
        st = sb("st", [P, CC, 2 * CHUNKS, 6])
        st1 = sb("st1", [P, CC, CHUNKS, 6])
        mv = sb("mv", [P, CC, 2])
        mom = sb("mom", [P, 2, CC])
        gm = sb("gm", [P, 2, CC])
        sm = sb("sm", [P, 12, CC])
        aff = sb("aff", [P, 2, CC])
        offall = sb("offall", [P, TILES, OFFS])
        widx = sb("widx", [P, TILES, TAPS], I32)
        wall = sb("wall", [P, 4, TILES, TAPS])
        idxc = sb("idxc", [P, CT * TAPS], I32)
        wcur = sb("wcur", [P, 4, CT * TAPS])
        corners = [sb(f"corners{i}", [P, 4 * C]) for i in range(4)]
        vpix = [sb(f"vpix{i}", [P, ST, C]) for i in range(2)]
        vT = [sb(f"vT{i}", [P, CC, ST * P]) for i in range(2)]
        yc = [sb(f"yc{i}", [P, CC, ST * P]) for i in range(2)]

        banks = [ctx.enter_context(nc.psum_tensor(n, [P, NC], F32))
                 for n in ("ps_s0", "ps_s1", "ps_s2", "ps_pv", "ps_sum", "ps_max", "ps_vt", "ps_y")]
        S = banks[0:3]
        PV, SUM, MX, VT, Y = banks[3:8]

        sems = []

        def sem(name):
            s = ctx.enter_context(nc.semaphore(name))
            sems.append(s)
            return s

        loaded = sem("loaded")
        chain = sem("chain")
        mom_ready, grp_ready = sem("mom_ready"), sem("grp_ready")
        root_in, root_out = sem("root_in"), sem("root_out")
        aff_ready = sem("aff_ready")
        norm_act, norm_dve = sem("norm_act"), sem("norm_dve")
        qk_ps, qk_hi, qk_rest, qk_mid, qk_lo = (sem(n) for n in ("qk_ps", "qk_hi", "qk_rest", "qk_mid", "qk_lo"))
        stored = [sem(f"stored{i}") for i in range(4)]
        v_ps, v_sb = sem("v_ps"), sem("v_sb")
        ones_set = sem("ones_set")
        q_loaded = sem("q_loaded")
        mx_full, mx_read, neg_ready = sem("mx_full"), sem("mx_read"), sem("neg_ready")
        s_full, exp_done, p_used = (sem(n) for n in ("s_full", "exp_done", "p_used"))
        attn_ready, proj_full, x1_ready = sem("attn_ready"), sem("proj_full"), sem("x1_ready")
        idx_ready, w_ready = sem("idx_ready"), sem("w_ready")
        gathered = [sem(f"gathered{i}") for i in range(4)]
        blended, vt_full, vt_sb, conv_done, y_ready = (
            sem(n) for n in ("blended", "vt_full", "vt_sb", "conv_done", "y_ready"))
        ring_zero, off_full, off_sb, offT_full, offT_sb = (
            sem(n) for n in ("ring_zero", "off_full", "off_sb", "offT_full", "offT_sb"))
        px_full, px_act, px_dve = sem("px_full"), sem("px_act"), sem("px_dve")
        in_loaded = [sem("in_loaded0"), sem("in_loaded1")]
        out_ready = [sem("out_ready0"), sem("out_ready1")]

        def clear():
            nc.gpsimd.dma_reset(range(gathered[0].num, gathered[-1].num + 1))
            nc.gpsimd.sem_clear(range(sems[0].num, sems[-1].num + 1))
            nc.all_engine_barrier()

        def linker(dve):
            n = [0]

            def link(ins):
                n[0] += 1
                ins.then_inc(chain, 1)
                dve.wait_ge(chain, n[0])
            return link

        def dve_moments(link, stats, mom_count):
            for c in range(CC):
                link(nc.vector.bn_aggr(mv[:, c, :], stats[:, c, :, :].rearrange("p a s -> p (a s)")))
            link(nc.vector.tensor_tensor(mom[:, 1, :], mv[:, :, 0], mv[:, :, 0], ALU.mult))
            link(nc.vector.tensor_tensor(mom[:, 1, :], mom[:, 1, :], mv[:, :, 1], ALU.add))
            nc.vector.tensor_copy(mom[:, 0, :], mv[:, :, 0]).then_inc(mom_ready, 1)

        def pe_group_means(pe):
            pe.wait_ge(mom_ready, 1)
            nc.tensor.matmul(MX[:, 0:2 * CC], gmean[:, :], mom[:, :, :].rearrange("p s c -> p (s c)"),
                             start=True, stop=True).then_inc(grp_ready, 1)

        def act_root(act, n):
            act.wait_ge(root_in, n)
            nc.scalar.activation(sm[:, 1, :], sm[:, 0, :], ACT.Sqrt).then_inc(root_out, 1)

        def dve_rsqrt(dve, link, out_ap, n):
            dve.wait_ge(root_out, n)
            link(nc.vector.reciprocal(sm[:, 2, :], sm[:, 1, :]))
            link(nc.vector.tensor_tensor(sm[:, 3, :], sm[:, 2, :], sm[:, 2, :], ALU.mult))
            link(nc.vector.tensor_tensor(sm[:, 3, :], sm[:, 3, :], sm[:, 0, :], ALU.mult))
            link(nc.vector.tensor_scalar(sm[:, 3, :], sm[:, 3, :], -0.5, 1.5, ALU.mult, ALU.add))
            link(nc.vector.tensor_tensor(out_ap, sm[:, 3, :], sm[:, 2, :], ALU.mult))

        def dve_group_var(dve, link):
            dve.wait_ge(grp_ready, 1)
            link(nc.vector.tensor_copy(gm[:, :, :].rearrange("p s c -> p (s c)"), MX[:, 0:2 * CC]))
            link(nc.vector.tensor_tensor(sm[:, 4, :], gm[:, 0, :], gm[:, 0, :], ALU.mult))
            link(nc.vector.tensor_tensor(sm[:, 5, :], gm[:, 1, :], sm[:, 4, :], ALU.subtract))
            nc.vector.tensor_scalar(sm[:, 0, :], sm[:, 5, :], EPS, None, ALU.add).then_inc(root_in, 1)

        def dve_affine(link, rate, weight, bias):
            if weight is not None:
                link(nc.vector.tensor_tensor(aff[:, 0, :], rate, weight, ALU.mult))
            link(nc.vector.tensor_tensor(sm[:, 7, :], gm[:, 0, :], aff[:, 0, :], ALU.mult))
            if bias is None:
                nc.vector.tensor_scalar(aff[:, 1, :], sm[:, 7, :], -1.0, None, ALU.mult).then_inc(aff_ready, 1)
            else:
                nc.vector.tensor_tensor(aff[:, 1, :], bias, sm[:, 7, :], ALU.subtract).then_inc(aff_ready, 1)

        with nc.Block() as block:
            @block.sync
            def _(sp):
                loads = [(ident[:, :], ident_c), (gmean[:, :], gmean_c), (allmean[:, :], all_c),
                         (base[:, :, :], base_c), (wqkv[:, :, :], wqkvT), (wout[:, :], woutT),
                         (wc[:, :, :], wcT)]
                loads += [(vecs[:, i, :], v) for i, v in enumerate((gamma, beta, bout, bconv, gnw, gnb))]
                for dst, src in loads:
                    sp.dma_start(dst, src).then_inc(loaded, 16)
                sp.wait_ge(ones_set, 3)
                sp.dma_start(woff[:, :, 0:OFFS], woffT).then_inc(loaded, 16)
                for t in range(4):
                    sp.dma_start(v_boff[DH * t:DH * t + OFFS, :], boff).then_inc(loaded, 16)
                n = 16 * (len(loads) + 5)
                sp.wait_ge(ring_zero, 1)
                rows = LEAD + HP * WP - PTILES * P
                sp.dma_start(tab[PTILES * P:LEAD + HP * WP, :], corners[0][0:rows, :]).then_inc(stored[0], 16)
                sp.dma_start(tab[0:LEAD, :], corners[0][0:LEAD, :]).then_inc(stored[0], 16)
                sp.wait_ge(stored[0], 32)
                sp.wait_ge(loaded, n)

            @block.gpsimd
            def _(pool):
                nc.gpsimd.memset(ones[:, :], 1.0).then_inc(ones_set, 1)
                nc.gpsimd.memset(woff[:, :, :], 0.0).then_inc(ones_set, 1)
                nc.gpsimd.memset(v_boff[:, :], 0.0).then_inc(ones_set, 1)
                nc.gpsimd.memset(corners[0][:, :], 0.0).then_inc(ring_zero, 1)

            @block.vector
            def _(dve):
                dve.wait_ge(loaded, 16 * 18)
                nc.vector.tensor_copy(identb[:, :], ident[:, :]).then_inc(chain, 1)
        clear()

        def qkv(b):
            with nc.Block() as block:
                @block.sync
                def _(sp):
                    for c in range(CC):
                        sp.dma_start(xs[:, c, :], xv[b, :, c, :]).then_inc(loaded, 16)
                    for i in range(2 * CHUNKS):
                        which, n = divmod(i, CHUNKS)
                        sp.wait_ge(qk_lo, i + 1)
                        sp.dma_start(qkp[which, :, :, n * NC:(n + 1) * NC].rearrange("r p n -> p r n"),
                                     parts[i % 2][:, :, :]).then_inc(stored[i % 2], 16)
                    for i in range(2):
                        sp.wait_ge(stored[i], 16 * CHUNKS)
                    sp.wait_ge(v_ps, JT // 4)
                    for r, part in enumerate((0, 1, 0, 1)):
                        sp.dma_start(kA[DH * r:DH * (r + 1), :, :],
                                     qkp[1, part, :, :].rearrange("(h c) j -> c h j", h=HEADS)).then_inc(loaded, 16)
                    for r, part in enumerate((2, 0)):
                        sp.dma_start(kB[DH * r:DH * (r + 1), :, :],
                                     qkp[1, part, :, :].rearrange("(h c) j -> c h j", h=HEADS)).then_inc(loaded, 16)
                    sp.wait_ge(loaded, 16 * (CC + 6))

                @block.gpsimd
                def _(pool):
                    pool.wait_ge(v_ps, JT // 4)
                    nc.gpsimd.memset(kB[2 * DH:2 * DH + 3, :, :], 1.0).then_inc(ones_set, 1)

                @block.vector
                def _(dve):
                    link = linker(dve)
                    dve.wait_ge(loaded, 16 * CC)
                    for c in range(CC):
                        for n in range(CHUNKS):
                            ins = nc.vector.bn_stats(st1[:, c, n, :], xs[:, c, n * NC:(n + 1) * NC])
                    link(ins)
                    dve_moments(link, st1, 1)
                    dve_group_var(dve, link)
                    dve_rsqrt(dve, link, sm[:, 6, :], 1)
                    link(nc.vector.tensor_tensor(sm[:, 8, :], sm[:, 6, :], sm[:, 6, :], ALU.mult))
                    nc.vector.tensor_tensor(sm[:, 9, :], sm[:, 8, :], sm[:, 5, :], ALU.mult).then_inc(mom_ready, 1)
                    dve.wait_ge(grp_ready, 2)
                    link(nc.vector.reduce_sum(sm[:, 10, 0:1], VT[:, 0:CC], AX.X))
                    for c in range(CC):
                        ins = nc.vector.tensor_scalar(sm[:, 0, c:c + 1], sm[:, 10, 0:1], EPS, None, ALU.add)
                        if c == CC - 1:
                            ins.then_inc(root_in, 1)
                    dve_rsqrt(dve, link, sm[:, 8, :], 2)
                    link(nc.vector.tensor_tensor(sm[:, 9, :], sm[:, 6, :], sm[:, 8, :], ALU.mult))
                    dve_affine(link, sm[:, 9, :], v_gamma, v_beta)
                    dve.wait_ge(aff_ready, 1)
                    nc.vector.tensor_scalar(xs[:, 1, :], xs[:, 1, :], aff[:, 0, 1:2], aff[:, 1, 1:2],
                                            ALU.mult, ALU.add).then_inc(norm_dve, 1)

                    def rest(i):
                        dve.wait_ge(qk_hi, i + 1)
                        nc.vector.tensor_tensor(ptmp[i % 2][:, :], S[i % 2][:, :], parts[i % 2][:, 0, :],
                                                ALU.subtract).then_inc(qk_rest, 1)

                    def low(i):
                        dve.wait_ge(qk_mid, i + 1)
                        nc.vector.tensor_tensor(parts[i % 2][:, 2, :], ptmp[i % 2][:, :], parts[i % 2][:, 1, :],
                                                ALU.subtract).then_inc(qk_lo, 1)
                    for i in range(2 * CHUNKS):
                        rest(i)
                        if i:
                            low(i - 1)
                    low(2 * CHUNKS - 1)

                @block.scalar
                def _(act):
                    act_root(act, 1)
                    act_root(act, 2)
                    act.wait_ge(aff_ready, 1)
                    nc.scalar.activation(xs[:, 0, :], xs[:, 0, :], ACT.Identity, bias=aff[:, 1, 0:1],
                                         scale=aff[:, 0, 0:1]).then_inc(norm_act, 1)

                    def mid(i):
                        act.wait_ge(qk_rest, i + 1)
                        nc.scalar.activation(parts[i % 2][:, 1, :], ptmp[i % 2][:, :], ACT.Copy).then_inc(qk_mid, 1)
                    for i in range(2 * CHUNKS):
                        act.wait_ge(qk_ps, i + 1)
                        if i >= 2:
                            act.wait_ge(stored[i % 2], 16 * (i // 2))
                        nc.scalar.activation(parts[i % 2][:, 0, :], S[i % 2][:, :], ACT.Copy).then_inc(qk_hi, 1)
                        if i:
                            mid(i - 1)
                    mid(2 * CHUNKS - 1)
                    for i in range(JT // 4):
                        act.wait_ge(v_ps, i + 1)
                        nc.scalar.activation(vsb[:, 4 * i:4 * i + 4, :].rearrange("p j c -> p (j c)"),
                                             (S[2], PV)[i % 2][:, :], ACT.Copy).then_inc(v_sb, 1)

                @block.tensor
                def _(pe):
                    pe_group_means(pe)
                    pe.wait_ge(mom_ready, 2)
                    nc.tensor.matmul(VT[:, 0:CC], allmean[:, :], sm[:, 9, :], start=True, stop=True)\
                        .then_inc(grp_ready, 1)
                    pe.wait_ge(norm_act, 1)
                    pe.wait_ge(norm_dve, 1)
                    for i in range(2 * CHUNKS):
                        which, n = divmod(i, CHUNKS)
                        if i >= 2:
                            pe.wait_ge(qk_rest, i - 1)
                        for c in range(CC):
                            ins = nc.tensor.matmul(S[i % 2][:, :], wqkv[:, c, which * HID:(which + 1) * HID],
                                                   xs[:, c, n * NC:(n + 1) * NC], start=c == 0, stop=c == CC - 1)
                        ins.then_inc(qk_ps, 1)
                    for i in range(JT // 4):
                        if i >= 2:
                            pe.wait_ge(v_sb, i - 1)
                        for q in range(4):
                            j = 4 * i + q
                            for c in range(CC):
                                ins = nc.tensor.matmul((S[2], PV)[i % 2][:, q * P:(q + 1) * P],
                                                       xs[:, c, j * P:(j + 1) * P], wqkv[:, c, 2 * HID:3 * HID],
                                                       start=c == 0, stop=c == CC - 1)
                        ins.then_inc(v_ps, 1)
            clear()

        def load_q(sp, n):
            cols = bass.ds(n * NC, NC)
            for r, part in enumerate((0, 0, 1, 1)):
                sp.dma_start(qnA[DH * r:DH * (r + 1), :, :],
                             qkp[0, part, :, cols].rearrange("(h c) j -> c h j", h=HEADS)).then_inc(q_loaded, 16)
            for r, part in enumerate((0, 2)):
                sp.dma_start(qnB[DH * r:DH * (r + 1), :, :],
                             qkp[0, part, :, cols].rearrange("(h c) j -> c h j", h=HEADS)).then_inc(q_loaded, 16)

        def pe_max(pe, u):
            t, h, j = u // (HEADS * CHUNKS), u // CHUNKS % HEADS, u % CHUNKS
            if u:
                pe.wait_ge(mx_read, u)
            nc.tensor.matmul(MX[:, :], qnA[:, h, t * P:(t + 1) * P], kA[:, h, j * NC:(j + 1) * NC],
                             start=True, stop=True).then_inc(mx_full, 1)

        def dve_max(dve, u):
            dve.wait_ge(mx_full, u + 1)
            nc.vector.reduce_max(mx[:, u // CHUNKS, u % CHUNKS:u % CHUNKS + 1], MX[:, :], AX.X).then_inc(mx_read, 1)

        def dve_neg(dve, link):
            dve.wait_ge(mx_read, MAX_UNITS)
            link(nc.vector.reduce_max(neg[:, :], mx[:, :, :], AX.X))
            link(nc.vector.tensor_scalar(neg[:, :], neg[:, :], -1.0, None, ALU.mult))
            link(nc.vector.tensor_copy(negp[:, :, 0], neg[:, :]))
            link(nc.vector.tensor_tensor(neg2[:, :], neg[:, :], negp[:, :, 0], ALU.subtract))
            link(nc.vector.tensor_copy(negp[:, :, 1], neg2[:, :]))
            nc.vector.tensor_tensor(negp[:, :, 2], neg2[:, :], negp[:, :, 1], ALU.subtract).then_inc(neg_ready, 1)

        def pe_neg(pe, h):
            if h == 0:
                pe.wait_ge(neg_ready, 1)
            pe.wait_ge(mx_read, MAX_UNITS + h)
            for t in range(CT):
                ins = nc.tensor.matmul(MX[2 * DH:2 * DH + 3, t * P:(t + 1) * P], negp[:, t * HEADS + h, :],
                                       identb[:, :], start=True, stop=True, tile_position=(0, 2 * DH))
            ins.then_inc(mx_full, 1)

        def dve_neg_rows(dve, h):
            dve.wait_ge(mx_full, MAX_UNITS + h + 1)
            nc.vector.tensor_copy(qnB[2 * DH:2 * DH + 3, h, :], MX[2 * DH:2 * DH + 3, :]).then_inc(mx_read, 1)

        def dve_take_q(dve):
            dve.wait_ge(mx_read, MAX_UNITS + HEADS)
            dve.wait_ge(q_loaded, 16 * 6)
            rows = 2 * DH + 3
            nc.vector.tensor_copy(qcA[:, :, :], qnA[:, :, :])
            nc.vector.tensor_copy(qcB[0:rows, :, :], qnB[0:rows, :, :])

        def first_max():
            with nc.Block() as block:
                @block.sync
                def _(sp):
                    load_q(sp, 0)
                    sp.wait_ge(q_loaded, 16 * 6)

                @block.tensor
                def _(pe):
                    pe.wait_ge(q_loaded, 16 * 6)
                    for u in range(MAX_UNITS):
                        pe_max(pe, u)
                    for h in range(HEADS):
                        pe_neg(pe, h)

                @block.vector
                def _(dve):
                    link = linker(dve)
                    for u in range(MAX_UNITS):
                        dve_max(dve, u)
                    dve_neg(dve, link)
                    for h in range(HEADS):
                        dve_neg_rows(dve, h)
                    dve_take_q(dve)
            clear()

        def chunk(b, ic, attn, nxt, conv):
            with nc.Block() as block:
                @block.sync
                def _(sp):
                    if nxt:
                        load_q(sp, ic + 1)
                    if attn:
                        sp.dma_start(xr[:, :, :], xv[b, :, :, bass.ds(ic * NC, NC)]).then_inc(loaded, 16)
                    if conv:
                        for s in range(SUBS):
                            sp.wait_ge(y_ready, CC * (s + 1))
                            sp.dma_start(ys[:, :, bass.ds(ic * NC + s * ST * P, ST * P)], yc[s][:, :, :])\
                                .then_inc(stored[1], 16)
                    if attn:
                        sp.wait_ge(x1_ready, CC)
                        sp.dma_start(x1s[b, :, :, bass.ds(ic * NC, NC)], xr[:, :, :]).then_inc(stored[0], 16)
                        sp.wait_ge(stored[0], 16)
                    if nxt:
                        sp.wait_ge(q_loaded, 16 * 6)
                    if conv:
                        sp.wait_ge(stored[1], 16 * SUBS)

                @block.gpsimd
                def _(pool):
                    if conv:
                        nc.gpsimd.tensor_copy(idxc[:, :], widx[:, :, :].rearrange("p t k -> p (t k)")
                                              [:, bass.ds(ic * CT * TAPS, CT * TAPS)]).then_inc(idx_ready, 1)
                        pool.wait_ge(idx_ready, 1)
                        for u in range(ST * STEPS):
                            s, i = divmod(u, ST)
                            col = (s // TAPS * ST + i) * TAPS + s % TAPS
                            if u >= 4:
                                pool.wait_ge(blended, u - 3)
                            nc.gpsimd.indirect_dma_start(
                                corners[u % 4][:, :], None, tab,
                                bass.IndirectOffsetOnAxis(ap=idxc[:, col:col + 1].bitcast(U32), axis=0))\
                                .then_inc(gathered[u % 4], 16)
                        for i in range(4):
                            pool.wait_ge(gathered[i], 16 * (ST * STEPS // 4))

                @block.scalar
                def _(act):
                    def evacuate(s):
                        act.wait_ge(vt_full, s + 1)
                        if s >= 2:
                            act.wait_ge(conv_done, s - 1)
                        nc.scalar.activation(vT[s % 2][:, :, :].rearrange("p c n -> p (c n)"), VT[:, :],
                                             ACT.Copy).then_inc(vt_sb, 1)

                    def finish(sub):
                        act.wait_ge(conv_done, TAPS * (sub + 1))
                        for o in range(CC):
                            nc.scalar.activation(yc[sub][:, o, :], Y[:, o * ST * P:(o + 1) * ST * P], ACT.Identity,
                                                 bias=v_bconv[:, o:o + 1]).then_inc(y_ready, 1)
                    for jt in range(JT):
                        if attn:
                            for h in range(HEADS):
                                u = jt * HEADS + h
                                act.wait_ge(s_full, u + 1)
                                if h == 0 and jt >= 2:
                                    act.wait_ge(p_used, jt - 1)
                                nc.scalar.activation(probs[jt % 2][:, h, :], S[u % 3][:, :], ACT.Exp,
                                                     scale=SCALE).then_inc(exp_done, 1)
                        s = step_of(jt) if conv else None
                        if s is not None:
                            evacuate(s)
                            if s == TAPS:
                                finish(0)
                    if conv:
                        finish(1)

                @block.vector
                def _(dve):
                    link = linker(dve)
                    linked = [0]

                    if conv:
                        nc.vector.tensor_copy(wcur[:, :, :], wall[:, :, :, :].rearrange("p q t k -> p q (t k)")
                                              [:, :, bass.ds(ic * CT * TAPS, CT * TAPS)]).then_inc(w_ready, 1)
                        dve.wait_ge(w_ready, 1)

                    def y_stats(sub):
                        dve.wait_ge(y_ready, CC * (sub + 1))
                        for o in range(CC):
                            nc.vector.bn_stats(st[:, o, bass.ds(ic * SUBS + sub, 1), :].rearrange("p a s -> p (a s)"),
                                               yc[sub][:, o, :])

                    blend_chain = w_ready

                    def blend(s):
                        if s >= 2:
                            dve.wait_ge(vt_full, s - 1)
                        for q in range(4):
                            for i in range(ST):
                                u = s * ST + i
                                col = (s // TAPS * ST + i) * TAPS + s % TAPS
                                v = vpix[s % 2][:, i, :]
                                g = corners[u % 4][:, q * C:(q + 1) * C]
                                w = wcur[:, q, col:col + 1]
                                if q == 0:
                                    dve.wait_ge(gathered[u % 4], 16 * (u // 4 + 1))
                                    nc.vector.tensor_scalar(v, g, w, None, ALU.mult).then_inc(blend_chain, 1)
                                else:
                                    dve.wait_ge(blend_chain, 1 + (s * 3 + q - 1) * ST + i + 1)
                                    nc.vector.scalar_tensor_tensor(v, g, w, v, ALU.mult, ALU.add)\
                                        .then_inc(blended if q == 3 else blend_chain, 1)

                    for jt in range(JT):
                        s = step_of(jt) if conv else None
                        if s is not None:
                            blend(s)
                            if s == TAPS + 1:
                                y_stats(0)
                        if nxt and jt >= MAX_FROM:
                            u0 = (jt - MAX_FROM) * MAX_PER_JT
                            for u in range(u0, min(u0 + MAX_PER_JT, MAX_UNITS)):
                                dve_max(dve, u)
                            if jt == NEG_AT - 1:
                                dve_neg(dve, link)
                            if jt >= NEG_AT:
                                dve_neg_rows(dve, jt - NEG_AT)
                    if conv:
                        y_stats(1)
                    if attn:
                        dve.wait_ge(p_used, JT)
                        nc.vector.reciprocal(rsum[:, :], SUM[:, :]).then_inc(attn_ready, 1)
                        dve.wait_ge(attn_ready, 1)
                        nc.vector.tensor_tensor(an[:, :], PV[:, :], rsum[:, :], ALU.mult).then_inc(attn_ready, 1)
                        if nxt:
                            dve_take_q(dve)
                        dve.wait_ge(loaded, 16)
                        for o in range(CC):
                            dve.wait_ge(proj_full, o + 1)
                            nc.vector.scalar_tensor_tensor(xr[:, o, :], S[o][:, :], v_bout[:, o:o + 1], xr[:, o, :],
                                                           ALU.add, ALU.add).then_inc(x1_ready, 1)
                        for o in range(CC):
                            dve.wait_ge(x1_ready, o + 1)
                            nc.vector.bn_stats(st1[:, o, bass.ds(ic, 1), :].rearrange("p a s -> p (a s)"), xr[:, o, :])

                @block.tensor
                def _(pe):
                    def turn(s):
                        pe.wait_ge(blended, ST * (s + 1))
                        if s:
                            pe.wait_ge(vt_sb, s)
                        for c in range(CC):
                            for i in range(ST):
                                ins = nc.tensor.transpose(VT[:, (c * ST + i) * P:(c * ST + i + 1) * P],
                                                          vpix[s % 2][:, i, c * P:(c + 1) * P], ident[:, :])
                        ins.then_inc(vt_full, 1)

                    def convolve(s):
                        sub, tap = divmod(s, TAPS)
                        pe.wait_ge(vt_sb, s + 1)
                        if tap == 0 and sub:
                            pe.wait_ge(y_ready, CC * sub)
                        for c in range(CC):
                            for o in range(CC):
                                ins = nc.tensor.matmul(Y[:, o * ST * P:(o + 1) * ST * P],
                                                       wc[:, c * TAPS + tap, o * P:(o + 1) * P], vT[s % 2][:, c, :],
                                                       start=tap == 0 and c == 0 and o == 0,
                                                       stop=tap == TAPS - 1 and c == CC - 1, skip_group_check=True)
                        ins.then_inc(conv_done, 1)

                    def scores(jt, h):
                        u = jt * HEADS + h
                        if u >= 3:
                            pe.wait_ge(exp_done, u - 2)
                        keys = slice(jt * P, (jt + 1) * P)
                        rows = 2 * DH + 3
                        nc.tensor.matmul(S[u % 3][:, :], kA[:, h, keys], qcA[:, h, :], start=True, stop=False)
                        nc.tensor.matmul(S[u % 3][:, :], kB[0:rows, h, keys], qcB[0:rows, h, :], start=False,
                                         stop=True).then_inc(s_full, 1)

                    def weigh(jt):
                        pe.wait_ge(exp_done, HEADS * (jt + 1))
                        for left, acc in ((None, SUM), (vsb, PV)):
                            for h in range(HEADS):
                                band = slice(h * DH, (h + 1) * DH)
                                lhs = ones[:, :] if left is None else vsb[:, jt, band]
                                ins = nc.tensor.matmul(acc[band, :], lhs, probs[jt % 2][:, h, :], start=jt == 0,
                                                       stop=jt == JT - 1, tile_position=(0, h * DH),
                                                       skip_group_check=True)
                        ins.then_inc(p_used, 1)

                    if nxt:
                        pe.wait_ge(q_loaded, 16 * 6)
                    for jt in range(JT):
                        units = []
                        if nxt and jt >= MAX_FROM:
                            u0 = (jt - MAX_FROM) * MAX_PER_JT
                            units = list(range(u0, min(u0 + MAX_PER_JT, MAX_UNITS)))
                        if attn:
                            for h in range(HEADS):
                                scores(jt, h)
                                if h and units:
                                    pe_max(pe, units.pop(0))
                        if attn and jt:
                            weigh(jt - 1)
                        for u in units:
                            pe_max(pe, u)
                        if nxt and jt >= NEG_AT:
                            pe_neg(pe, jt - NEG_AT)
                        s = step_of(jt) if conv else None
                        if s is not None:
                            turn(s)
                            if s:
                                convolve(s - 1)
                    if conv:
                        convolve(STEPS - 1)
                    if attn:
                        weigh(JT - 1)
                        pe.wait_ge(attn_ready, 2)
                        for o in range(CC):
                            nc.tensor.matmul(S[o][:, :], wout[:, o * P:(o + 1) * P], an[:, :], start=True,
                                             stop=True).then_inc(proj_full, 1)
            clear()

        def prepare(b):
            with nc.Block() as block:
                @block.sync
                def _(sp):
                    for c in range(CC):
                        sp.dma_start(xs[:, c, :], x1s[b, :, c, :]).then_inc(loaded, 16)
                    for g, m in enumerate(PGROUPS):
                        sp.wait_ge(px_act, g + 1)
                        sp.wait_ge(px_dve, min(g + 1, PTILES // 4))
                        for q in range(4):
                            first = LEAD + 4 * g * P - (q // 2 * WP + q % 2)
                            dst = tab[first:first + m * P, q * C:(q + 1) * C].rearrange("(t p) c -> p t c", p=P)
                            src = corners[g % 4][:, 0:m * C].rearrange("p (t c) -> p t c", t=m)
                            sp.dma_start(dst, src).then_inc(stored[g % 4], 16)
                    for i in range(4):
                        sp.wait_ge(stored[i], 64 * len(PGROUPS[i::4]))
                    sp.wait_ge(loaded, 16 * CC)

                @block.gpsimd
                def _(pool):
                    for c in range(CC):
                        nc.gpsimd.memset(h1[:, c, 0, :], 0.0)
                        nc.gpsimd.memset(h1[:, c, HP - 1, :], 0.0)
                        nc.gpsimd.memset(h1[:, c, 1:HP - 1, 0:1], 0.0)
                        nc.gpsimd.memset(h1[:, c, 1:HP - 1, WP - 1:WP], 0.0).then_inc(ring_zero, 1)

                @block.scalar
                def _(act):
                    act_root(act, 1)
                    act.wait_ge(aff_ready, 1)
                    act.wait_ge(loaded, 16 * CC)
                    nc.scalar.activation(h1[:, 0, 1:H + 1, 1:W + 1], xs[:, 0, :].rearrange("p (y x) -> p y x", x=W),
                                         ACT.Identity, bias=aff[:, 1, 0:1], scale=aff[:, 0, 0:1]).then_inc(norm_act, 1)
                    for r in range(2):
                        act.wait_ge(off_full, r + 1)
                        nc.scalar.activation(pflat[0][:, r * NC:(r + 1) * NC], S[r][:, :], ACT.Identity,
                                             bias=v_boff[:, :]).then_inc(off_sb, 1)
                    for j in range(0, PTILES // 2, 2):
                        if j >= 8:
                            act.wait_ge(stored[j // 2 % 4], 64 * (j // 8))
                        act.wait_ge(px_full, j + 1)
                        nc.scalar.activation(corners[j // 2 % 4][:, 0:NC], (SUM, MX, VT, Y)[j % 4][:, :],
                                             ACT.Copy).then_inc(px_act, 1)

                @block.tensor
                def _(pe):
                    pe_group_means(pe)
                    pe.wait_ge(norm_act, 1)
                    pe.wait_ge(norm_dve, 1)
                    pe.wait_ge(ring_zero, CC)
                    for r in range(2):
                        for c in range(CC):
                            for tap in range(TAPS):
                                ky, kx = divmod(tap, K)
                                for t in range(4):
                                    y0 = 8 * (4 * r + t) + ky
                                    ins = nc.tensor.matmul(S[r][DH * t:DH * (t + 1), :], woff[:, c * TAPS + tap, :],
                                                           h1[:, c, y0:y0 + 8, kx:kx + W],
                                                           start=c == 0 and tap == 0, stop=c == CC - 1 and tap == TAPS - 1,
                                                           tile_position=(0, DH * t), skip_group_check=True)
                        ins.then_inc(off_full, 1)
                    for r in range(2):
                        pe.wait_ge(off_sb, r + 1)
                        for q in range(4):
                            ins = nc.tensor.transpose((S[2], PV)[r][:, q * P:(q + 1) * P],
                                                      pflat[0][:, r * NC + q * P:r * NC + (q + 1) * P], ident[:, :])
                        ins.then_inc(offT_full, 1)
                    for j in range(PTILES // 2):
                        if j >= 4:
                            pe.wait_ge(px_dve if j % 2 else px_act, (j - 4) // 2 + 1)
                        for i in range(2):
                            for c in range(CC):
                                e0 = (2 * j + i) * P
                                ins = nc.tensor.transpose(
                                    (SUM, MX, VT, Y)[j % 4][:, (i * CC + c) * P:(i * CC + c + 1) * P],
                                    h1flat[:, c, e0:e0 + P], ident[:, :])
                        ins.then_inc(px_full, 1)

                @block.vector
                def _(dve):
                    link = linker(dve)
                    dve_moments(link, st1, 1)
                    dve_group_var(dve, link)
                    dve_rsqrt(dve, link, aff[:, 0, :], 1)
                    dve_affine(link, None, None, None)
                    dve.wait_ge(aff_ready, 1)
                    dve.wait_ge(loaded, 16 * CC)
                    nc.vector.tensor_scalar(h1[:, 1, 1:H + 1, 1:W + 1], xs[:, 1, :].rearrange("p (y x) -> p y x", x=W),
                                            aff[:, 0, 1:2], aff[:, 1, 1:2], ALU.mult, ALU.add).then_inc(norm_dve, 1)
                    for r in range(2):
                        dve.wait_ge(offT_full, r + 1)
                        link(nc.vector.tensor_copy(
                            offall[:, 16 * r:16 * (r + 1), :].rearrange("p (t q) o -> p q t o", t=4),
                            (S[2], PV)[r][:, :].rearrange("p (q t o) -> p q t o", q=4, t=4)[:, :, :, 0:OFFS]))
                    n = TILES * OFFS
                    flat = offall[:, :, :].rearrange("p t o -> p (t o)")
                    t0, t1, t2 = (pflat[1][:, i * n:(i + 1) * n] for i in range(3))
                    pos = flat
                    link(nc.vector.tensor_tensor(pos, flat, base[:, :, :].rearrange("p t o -> p (t o)"), ALU.add))
                    link(nc.vector.tensor_scalar(pos, pos, 0.0, float(HP - 1), ALU.max, ALU.min))
                    whole = t0.bitcast(I32)
                    link(nc.vector.tensor_copy(whole, pos))
                    link(nc.vector.tensor_copy(t1, whole))
                    link(nc.vector.tensor_tensor(t2, t1, pos, ALU.is_gt))
                    link(nc.vector.tensor_tensor(t1, t1, t2, ALU.subtract))
                    link(nc.vector.tensor_tensor(pos, pos, t1, ALU.subtract))
                    link(nc.vector.tensor_scalar(t2, pos, -1.0, 1.0, ALU.mult, ALU.add))
                    fy, fx = offall[:, :, 0:TAPS], offall[:, :, TAPS:OFFS]
                    far = t2.rearrange("p (t o) -> p t o", o=OFFS)
                    gy, gx = far[:, :, 0:TAPS], far[:, :, TAPS:OFFS]
                    low = t1.rearrange("p (t o) -> p t o", o=OFFS)
                    for q, (wy, wx) in enumerate(((gy, gx), (gy, fx), (fy, gx), (fy, fx))):
                        nc.vector.tensor_tensor(wall[:, q, :, :], wy, wx, ALU.mult)
                    t0v = t0.rearrange("p (t o) -> p t o", o=OFFS)[:, :, 0:TAPS]
                    link(nc.vector.scalar_tensor_tensor(t0v, low[:, :, 0:TAPS], float(WP), low[:, :, TAPS:OFFS],
                                                        ALU.mult, ALU.add))
                    link(nc.vector.tensor_scalar(t0v, t0v, float(LEAD), None, ALU.add))
                    link(nc.vector.tensor_copy(widx[:, :, :], t0v))
                    for j in range(1, PTILES // 2, 2):
                        if j >= 8:
                            dve.wait_ge(stored[j // 2 % 4], 64 * (j // 8))
                        dve.wait_ge(px_full, j + 1)
                        nc.vector.tensor_copy(corners[j // 2 % 4][:, NC:2 * NC],
                                              (SUM, MX, VT, Y)[j % 4][:, :]).then_inc(px_dve, 1)
            clear()

        def finish(b):
            with nc.Block() as block:
                bufs = [t.rearrange("p (a c n) -> p a c n", a=2, c=CC) for t in pflat]

                @block.sync
                def _(sp):
                    def load(n):
                        if n >= 2:
                            sp.wait_ge(stored[n % 2], 16 * (n // 2))
                        cols = slice(n * NC, (n + 1) * NC)
                        sp.dma_start(bufs[n % 2][:, 0, :, :], ys[:, :, cols]).then_inc(in_loaded[n % 2], 16)
                        sp.dma_start(bufs[n % 2][:, 1, :, :], x1s[b, :, :, cols]).then_inc(in_loaded[n % 2], 16)
                    load(0)
                    for n in range(CHUNKS):
                        if n + 1 < CHUNKS:
                            load(n + 1)
                        sp.wait_ge(out_ready[n % 2], CC * (n // 2 + 1))
                        sp.dma_start(ov[b, :, :, n * NC:(n + 1) * NC], bufs[n % 2][:, 0, :, :])\
                            .then_inc(stored[n % 2], 16)
                    for i in range(2):
                        sp.wait_ge(stored[i], 16 * CHUNKS // 2)

                @block.tensor
                def _(pe):
                    pe_group_means(pe)

                @block.scalar
                def _(act):
                    act_root(act, 1)
                    act.wait_ge(aff_ready, 1)
                    for n in range(CHUNKS):
                        act.wait_ge(in_loaded[n % 2], 32 * (n // 2 + 1))
                        for c in range(CC):
                            nc.scalar.activation(bufs[n % 2][:, 1, c, :], bufs[n % 2][:, 1, c, :], ACT.Identity,
                                                 bias=aff[:, 1, c:c + 1]).then_inc(norm_act, 1)

                @block.vector
                def _(dve):
                    link = linker(dve)
                    dve_moments(link, st, 1)
                    dve_group_var(dve, link)
                    dve_rsqrt(dve, link, sm[:, 6, :], 1)
                    dve_affine(link, sm[:, 6, :], v_gnw, v_gnb)
                    for n in range(CHUNKS):
                        dve.wait_ge(norm_act, CC * (n + 1))
                        for c in range(CC):
                            y = bufs[n % 2][:, 0, c, :]
                            nc.vector.scalar_tensor_tensor(y, y, aff[:, 0, c:c + 1], bufs[n % 2][:, 1, c, :],
                                                           ALU.mult, ALU.add).then_inc(out_ready[n % 2], 1)
            clear()

        def batch(b, conv):
            qkv(b)
            first_max()
            with nc.Fori(0, CHUNKS - 1) as ic:
                chunk(b, ic, True, True, conv)
            chunk(b, CHUNKS - 1, True, False, conv)
            if conv:
                finish(b - 1)
            prepare(b)

        batch(0, False)
        with nc.Fori(1, B) as b:
            batch(b, True)
        with nc.Fori(0, CHUNKS) as ic:
            chunk(None, ic, False, False, True)
        finish(B - 1)


def kernel(**inputs):
    import numpy as _np
    import concourse.bacc as _bacc
    from concourse import mybir as _mybir
    from concourse.bass_utils import run_bass_kernel_spmd as _run

    a = {k: _np.asarray(v) for k, v in inputs.items()}

    def halves(v):
        return v.reshape(CC, P).T

    px = _np.arange(N).reshape(TILES, P)
    base = _np.zeros((P, TILES, OFFS), _np.float32)
    for k in range(TAPS):
        base[:, :, k] = (px // W + k // K).T
        base[:, :, TAPS + k] = (px % W + k % K).T
    arrays = {
        "x": a["x"],
        "gamma": halves(a["L0_conv_gamma"]),
        "beta": halves(a["L0_conv_beta"]),
        "wqkvT": a["L0_conv_w_qkv"].T.reshape(CC, P, 3 * HID).transpose(1, 0, 2),
        "woutT": a["L0_conv_w_out"].T,
        "bout": halves(a["L0_conv_b_out"]),
        "woffT": a["L1_conv_w_off"].reshape(OFFS, CC, P, TAPS).transpose(2, 1, 3, 0).reshape(P, CC * TAPS, OFFS),
        "boff": a["L1_conv_b_off"].reshape(OFFS, 1),
        "wcT": a["L1_conv_w"].reshape(C, CC, P, TAPS).transpose(2, 1, 3, 0).reshape(P, CC * TAPS, C),
        "bconv": halves(a["L1_conv_b"]),
        "gnw": halves(a["L1_conv_gn_w"]),
        "gnb": halves(a["L1_conv_gn_b"]),
        "ident": _np.eye(P, dtype=_np.float32),
        "gmean": (_np.kron(_np.eye(P // GROUP), _np.ones((GROUP, GROUP))) / GROUP).astype(_np.float32),
        "allmean": _np.full((P, P), 1.0 / C, _np.float32),
        "base": base,
    }
    arrays = {k: _np.ascontiguousarray(v) for k, v in arrays.items()}
    nc = _bacc.Bacc("TRN2", target_bir_lowering=False, num_devices=1)
    args = [nc.dram_tensor(f"in_{k}", v.shape, _mybir.dt.float32, kind="ExternalInput").ap() for k, v in arrays.items()]
    out = nc.dram_tensor("out_0", (B, C, H, W), _mybir.dt.float32, kind="ExternalOutput").ap()
    build(nc, *args, out)
    r = _run(nc, [{f"in_{k}": v for k, v in arrays.items()}], core_ids=[0])
    return r.results[0]["out_0"]
```

```python
import concourse.bass as bass
from concourse import mybir
from contextlib import ExitStack

F32 = mybir.dt.float32
F16 = mybir.dt.float16
I32 = mybir.dt.int32
U32 = mybir.dt.uint32
RMAX = bass.bass_isa.ReduceOp.max
ACT = mybir.ActivationFunctionType
ALU = mybir.AluOpType
AX = mybir.AxisListType

B, C, H, W = 4, 256, 64, 64
P = 128
CC = C // P
N = H * W
NC = 512
CHUNKS = N // NC
HEADS, DH = 4, 32
HID = HEADS * DH
SCALE = DH ** -0.5
JT = N // P
K, TAPS = 3, 9
HP, WP = H + 2, W + 2
EPS = 1e-5
GROUP = C // 32
TILES = N // P
LEAD = WP + 1
PTILES = HP * WP // P
PGROUPS = [4] * (PTILES // 4) + [PTILES % 4]
OFFS = 2 * TAPS
CT = NC // P
SUBS = 2
STEPS = SUBS * TAPS
ST = CT // SUBS
MAX_UNITS = CT * HEADS * CHUNKS
MAX_PER_JT = 5
LIFT = 2.0 ** 11
ONE = 2.0 ** 15
ROWS = 3 * DH + 3
RING = 3
SUMG = 2
NCORN = 6
MAX_FROM = 1
NEG_AT = JT - HEADS


def step_of(jt):
    first, last = 2, JT - 2
    at = {first + s * (last - first) // STEPS: s for s in range(STEPS)}
    return at.get(jt)


def build(nc, x, gamma, beta, wqkvT, woutT, bout, woffT, boff, wcT, bconv, gnw, gnb,
          ident_c, gmean_c, all_c, base_c, out):
    xv = x.rearrange("b (cc p) h w -> b p cc (h w)", p=P)
    ov = out.rearrange("b (cc p) h w -> b p cc (h w)", p=P)
    qkp = nc.dram_tensor("qk_parts", (2, 2, HID, N), F16).ap()
    x1s = nc.dram_tensor("x1_scratch", (B, P, CC, N), F32).ap()
    ys = nc.dram_tensor("y_scratch", (P, CC, N), F32).ap()
    tab = nc.dram_tensor("corner_table", (LEAD + HP * WP, 4 * C), F32).ap()

    ctx = ExitStack()
    with ctx:
        def sb(name, shape, dt=F32):
            return ctx.enter_context(nc.sbuf_tensor(name, shape, dt))

        ident = sb("ident", [P, P])
        identh = sb("identh", [P, P], F16)
        gmean = sb("gmean", [P, P])
        allmean = sb("allmean", [P, P])
        ones = sb("ones", [P, DH])
        base = sb("base", [P, TILES, OFFS])
        wqkv = sb("wqkv", [P, CC, 3 * HID])
        wout = sb("wout", [P, C])
        woff = sb("woff", [P, CC * TAPS, DH])
        wc = sb("wc", [P, CC * TAPS, C])
        vecs = sb("vecs", [P, 6, CC])
        v_gamma, v_beta, v_bout, v_bconv, v_gnw, v_gnb = (vecs[:, i, :] for i in range(6))
        v_boff = sb("v_boff", [P, 1])

        kk = sb("kk", [P, HP * WP * CC * 2], F16)
        kst = kk[:, 0:HEADS * N].rearrange("p (h j) -> p h j", h=HEADS)
        qkf = kk[:, 0:2 * 2 * N].bitcast(F32).rearrange("p (w n) -> p w n", w=2)
        h1 = kk[:, :].bitcast(F32).rearrange("p (cc y x) -> p cc y x", cc=CC, x=WP)
        h1flat = h1.rearrange("p cc y x -> p cc (y x)")
        wide = sb("wide", [P, CC * N])
        xs = wide[:, :].rearrange("p (cc n) -> p cc n", cc=CC)
        quarter = [wide[:, i * HEADS * NC:(i + 1) * HEADS * NC] for i in range(4)]

        vsb = sb("vsb", [P, JT, HID])
        qn = sb("qn", [P, HEADS, NC], F16)
        qc = sb("qc", [P, HEADS, NC], F16)
        pflat = [sb(f"probs{i}", [P, HEADS * NC])[:, :] for i in range(2)] + [quarter[0]]
        probs = [t.rearrange("p (h n) -> p h n", h=HEADS) for t in pflat]
        psums = [t.rearrange("p (h n) -> p h n", h=HEADS) for t in quarter[1:3]]
        parts = [sb(f"parts{i}", [P, 2, NC], F16) for i in range(4)]
        amax = sb("amax", [P, 2, CHUNKS])
        amax2 = sb("amax2", [P, 2])
        pow2 = sb("pow2", [P, 2])
        lift = sb("lift", [P, 2])
        escale = sb("escale", [P, 1])
        mx = sb("mx", [P, CT * HEADS, CHUNKS])
        neg = sb("neg", [P, CT * HEADS])
        neg2 = sb("neg2", [P, CT * HEADS])
        negp = sb("negp", [P, CT * HEADS, 3], F16)
        rsum = sb("rsum", [P, NC])
        an = sb("an", [P, NC])
        xr = sb("xr", [P, CC, NC])
        st = sb("st", [P, CC, 2 * CHUNKS, 6])
        st1 = sb("st1", [P, CC, CHUNKS, 6])
        mv = sb("mv", [P, CC, 2])
        mom = sb("mom", [P, 2, CC])
        gm = sb("gm", [P, 2, CC])
        sm = sb("sm", [P, 12, CC])
        aff = sb("aff", [P, 2, CC])
        affx = sb("affx", [P, 2, CC])
        offall = sb("offall", [P, TILES, OFFS])
        widx = sb("widx", [P, TILES, TAPS], I32)
        wall = sb("wall", [P, 4, TILES, TAPS])
        idxc = sb("idxc", [P, CT * TAPS], I32)
        wcur = sb("wcur", [P, 4, CT * TAPS])
        corners = [sb(f"corners{i}", [P, 4 * C]) for i in range(4)]
        corners += [quarter[3][:, i * 4 * C:(i + 1) * 4 * C] for i in range(2)]
        vpix = [sb(f"vpix{i}", [P, ST, C]) for i in range(2)]
        vT = [sb(f"vT{i}", [P, CC, ST * P]) for i in range(2)]
        yc = [sb(f"yc{i}", [P, CC, ST * P]) for i in range(2)]

        ps = ctx.enter_context(nc.psum_tensor("ps", [P, 8, NC], F32))
        banks = [ps[:, i, :] for i in range(8)]
        S, MX = banks[0:2], banks[2:4]
        PV, SUM, VT, Y = banks[4:8]
        WIDE = [ps[:, 2 * i:2 * i + 2, :].rearrange("p b n -> p (b n)") for i in range(3)]
        VB = banks[6:8]

        sems = []

        def sem(name):
            s = ctx.enter_context(nc.semaphore(name))
            sems.append(s)
            return s

        loaded = sem("loaded")
        chain = sem("chain")
        mom_ready, grp_ready = sem("mom_ready"), sem("grp_ready")
        root_in, root_out = sem("root_in"), sem("root_out")
        aff_ready = sem("aff_ready")
        norm_act, norm_dve = sem("norm_act"), sem("norm_dve")
        qk_ps, qk_sb, qk_hi, qk_lo = (sem(n) for n in ("qk_ps", "qk_sb", "qk_hi", "qk_lo"))
        amax_read, amax_ready, amax_all, lift_ready = (
            sem(n) for n in ("amax_read", "amax_ready", "amax_all", "lift_ready"))
        x_loaded, k_loaded, px_stored = sem("x_loaded"), sem("k_loaded"), [sem(f"px_stored{i}") for i in range(4)]
        stored = [sem(f"stored{i}") for i in range(4)]
        v_ps, v_sb = sem("v_ps"), sem("v_sb")
        ones_set = sem("ones_set")
        q_loaded = sem("q_loaded")
        mx_full, mx_read, neg_ready = sem("mx_full"), sem("mx_read"), sem("neg_ready")
        s_full, exp_done, p_used = (sem(n) for n in ("s_full", "exp_done", "p_used"))
        attn_ready, proj_full, x1_ready = sem("attn_ready"), sem("proj_full"), sem("x1_ready")
        idx_ready, w_ready, blend_chain = sem("idx_ready"), sem("w_ready"), sem("blend_chain")
        sum_used, offT_read = sem("sum_used"), sem("offT_read")
        gathered = [sem(f"gathered{i}") for i in range(NCORN)]
        p_added, first_corner = sem("p_added"), sem("first_corner")
        blended, vt_full, vt_sb, conv_done, y_ready = (
            sem(n) for n in ("blended", "vt_full", "vt_sb", "conv_done", "y_ready"))
        ring_zero, off_full, off_sb, offT_full, offT_sb = (
            sem(n) for n in ("ring_zero", "off_full", "off_sb", "offT_full", "offT_sb"))
        px_full, px_act, px_dve = sem("px_full"), sem("px_act"), sem("px_dve")
        in_loaded = [sem("in_loaded0"), sem("in_loaded1")]
        out_ready = [sem("out_ready0"), sem("out_ready1")]

        def clear():
            nc.gpsimd.dma_reset(range(gathered[0].num, gathered[-1].num + 1))
            nc.gpsimd.sem_clear(range(sems[0].num, sems[-1].num + 1))
            nc.all_engine_barrier()

        def linker(dve):
            n = [0]

            def link(ins):
                n[0] += 1
                ins.then_inc(chain, 1)
                dve.wait_ge(chain, n[0])
            return link

        def dve_moments(link, stats):
            for c in range(CC):
                link(nc.vector.bn_aggr(mv[:, c, :], stats[:, c, :, :].rearrange("p a s -> p (a s)")))
            link(nc.vector.tensor_tensor(mom[:, 1, :], mv[:, :, 0], mv[:, :, 0], ALU.mult))
            link(nc.vector.tensor_tensor(mom[:, 1, :], mom[:, 1, :], mv[:, :, 1], ALU.add))
            nc.vector.tensor_copy(mom[:, 0, :], mv[:, :, 0]).then_inc(mom_ready, 1)

        def pe_group_means(pe, n):
            pe.wait_ge(mom_ready, n)
            nc.tensor.matmul(VT[:, 0:2 * CC], gmean[:, :], mom[:, :, :].rearrange("p s c -> p (s c)"),
                             start=True, stop=True).then_inc(grp_ready, 1)

        def act_root(act, n):
            act.wait_ge(root_in, n)
            nc.scalar.activation(sm[:, 1, :], sm[:, 0, :], ACT.Sqrt).then_inc(root_out, 1)

        def dve_rsqrt(dve, link, out_ap, n):
            dve.wait_ge(root_out, n)
            link(nc.vector.reciprocal(sm[:, 2, :], sm[:, 1, :]))
            link(nc.vector.tensor_tensor(sm[:, 3, :], sm[:, 2, :], sm[:, 2, :], ALU.mult))
            link(nc.vector.tensor_tensor(sm[:, 3, :], sm[:, 3, :], sm[:, 0, :], ALU.mult))
            link(nc.vector.tensor_scalar(sm[:, 3, :], sm[:, 3, :], -0.5, 1.5, ALU.mult, ALU.add))
            link(nc.vector.tensor_tensor(out_ap, sm[:, 3, :], sm[:, 2, :], ALU.mult))

        def dve_group_var(dve, link, n):
            dve.wait_ge(grp_ready, n)
            link(nc.vector.tensor_copy(gm[:, :, :].rearrange("p s c -> p (s c)"), VT[:, 0:2 * CC]))
            link(nc.vector.tensor_tensor(sm[:, 4, :], gm[:, 0, :], gm[:, 0, :], ALU.mult))
            link(nc.vector.tensor_tensor(sm[:, 5, :], gm[:, 1, :], sm[:, 4, :], ALU.subtract))
            nc.vector.tensor_scalar(sm[:, 0, :], sm[:, 5, :], EPS, None, ALU.add).then_inc(root_in, 1)

        def dve_affine(link, dst, rate, weight, bias, done):
            if weight is not None:
                link(nc.vector.tensor_tensor(dst[:, 0, :], rate, weight, ALU.mult))
            link(nc.vector.tensor_tensor(sm[:, 7, :], gm[:, 0, :], dst[:, 0, :], ALU.mult))
            if bias is None:
                nc.vector.tensor_scalar(dst[:, 1, :], sm[:, 7, :], -1.0, None, ALU.mult).then_inc(done, 1)
            else:
                nc.vector.tensor_tensor(dst[:, 1, :], bias, sm[:, 7, :], ALU.subtract).then_inc(done, 1)

        with nc.Block() as block:
            @block.sync
            def _(sp):
                loads = [(ident[:, :], ident_c), (gmean[:, :], gmean_c), (allmean[:, :], all_c),
                         (base[:, :, :], base_c), (wqkv[:, :, :], wqkvT), (wout[:, :], woutT),
                         (wc[:, :, :], wcT)]
                loads += [(vecs[:, i, :], v) for i, v in enumerate((gamma, beta, bout, bconv, gnw, gnb))]
                for dst, src in loads:
                    sp.dma_start(dst, src).then_inc(loaded, 16)
                sp.wait_ge(ones_set, 3)
                sp.dma_start(woff[:, :, 0:OFFS], woffT).then_inc(loaded, 16)
                for t in range(4):
                    sp.dma_start(v_boff[DH * t:DH * t + OFFS, :], boff).then_inc(loaded, 16)
                n = 16 * (len(loads) + 5)
                sp.wait_ge(ring_zero, 1)
                rows = LEAD + HP * WP - PTILES * P
                sp.dma_start(tab[PTILES * P:LEAD + HP * WP, :], corners[0][0:rows, :]).then_inc(stored[0], 16)
                sp.dma_start(tab[0:LEAD, :], corners[0][0:LEAD, :]).then_inc(stored[0], 16)
                sp.wait_ge(stored[0], 32)
                sp.wait_ge(loaded, n)

            @block.gpsimd
            def _(pool):
                nc.gpsimd.memset(ones[:, :], 1.0).then_inc(ones_set, 1)
                nc.gpsimd.memset(woff[:, :, :], 0.0).then_inc(ones_set, 1)
                nc.gpsimd.memset(v_boff[:, :], 0.0).then_inc(ones_set, 1)
                nc.gpsimd.memset(corners[0][:, :], 0.0).then_inc(ring_zero, 1)

            @block.vector
            def _(dve):
                dve.wait_ge(loaded, 16 * 18)
                nc.vector.tensor_copy(identh[:, :], ident[:, :]).then_inc(chain, 1)
        clear()

        def load_q(sp, n):
            cols = bass.ds(n * NC, NC)
            for r, part in enumerate((0, 0, 1)):
                sp.dma_start(qn[DH * r:DH * (r + 1), :, :],
                             qkp[0, part, :, cols].rearrange("(h c) j -> c h j", h=HEADS)).then_inc(q_loaded, 16)

        def pe_max(pe, u):
            t, h, j = u // (HEADS * CHUNKS), u // CHUNKS % HEADS, u % CHUNKS
            if u >= 2:
                pe.wait_ge(mx_read, u - 1)
            nc.tensor.matmul(MX[u % 2], qn[0:3 * DH, h, t * P:(t + 1) * P], kst[0:3 * DH, h, j * NC:(j + 1) * NC],
                             start=True, stop=True).then_inc(mx_full, 1)

        def dve_max(dve, u):
            dve.wait_ge(mx_full, u + 1)
            nc.vector.reduce_max(mx[:, u // CHUNKS, u % CHUNKS:u % CHUNKS + 1], MX[u % 2], AX.X).then_inc(mx_read, 1)

        def dve_neg(dve, link, units, per_row):
            dve.wait_ge(mx_read, units)
            link(nc.vector.reduce_max(neg[:, :], mx[:, :, 0:per_row], AX.X))
            link(nc.vector.tensor_scalar(neg[:, :], neg[:, :], -1.0 / ONE, None, ALU.mult))
            link(nc.vector.tensor_copy(negp[:, :, 0], neg[:, :]))
            link(nc.vector.tensor_tensor(neg2[:, :], neg[:, :], negp[:, :, 0], ALU.subtract))
            link(nc.vector.tensor_copy(negp[:, :, 1], neg2[:, :]))
            nc.vector.tensor_tensor(negp[:, :, 2], neg2[:, :], negp[:, :, 1], ALU.subtract).then_inc(neg_ready, 1)

        def pe_neg(pe, h, units):
            if h == 0:
                pe.wait_ge(neg_ready, 1)
            if h >= 2:
                pe.wait_ge(mx_read, units + h - 1)
            for t in range(CT):
                ins = nc.tensor.matmul(MX[h % 2][3 * DH:ROWS, t * P:(t + 1) * P], negp[:, t * HEADS + h, :],
                                       identh[:, :], start=True, stop=True, tile_position=(0, 3 * DH))
            ins.then_inc(mx_full, 1)

        def dve_neg_rows(dve, h, units):
            dve.wait_ge(mx_full, units + h + 1)
            nc.vector.tensor_copy(qn[3 * DH:ROWS, h, :], MX[h % 2][3 * DH:ROWS, :]).then_inc(mx_read, 1)

        def dve_take_q(dve, units):
            dve.wait_ge(mx_read, units + HEADS)
            dve.wait_ge(q_loaded, 16 * 3)
            nc.vector.tensor_copy(qc[0:ROWS, :, :], qn[0:ROWS, :, :])

        PAIRS = CHUNKS // 2
        PUNITS = CT * HEADS * PAIRS
        VUNITS = JT // 4

        def first_max(b, fb):
            with nc.Block() as block:
                @block.sync
                def _(sp):
                    if b is not None:
                        for r, part in enumerate((0, 1, 0)):
                            sp.dma_start(kst[DH * r:DH * (r + 1), :, :],
                                         qkp[1, part, :, :].rearrange("(h c) j -> c h j", h=HEADS)).then_inc(k_loaded, 16)
                        load_q(sp, 0)
                    if fb is not None:
                        finish_loads(sp, fb)
                    if b is not None:
                        sp.wait_ge(k_loaded, 16 * 3)
                        sp.wait_ge(q_loaded, 16 * 3)

                @block.gpsimd
                def _(pool):
                    if b is not None:
                        nc.gpsimd.memset(kst[3 * DH:ROWS, :, :], ONE).then_inc(ones_set, 1)

                @block.tensor
                def _(pe):
                    if fb is not None:
                        pe_group_means(pe, 1)

                    def values(i):
                        if fb is not None and i == 0:
                            pe.wait_ge(root_in, 1)
                        if i >= 2:
                            pe.wait_ge(v_sb, i - 1)
                        for q in range(4):
                            j = 4 * i + q
                            for c in range(CC):
                                ins = nc.tensor.matmul(VB[i % 2][:, q * P:(q + 1) * P], xs[:, c, j * P:(j + 1) * P],
                                                       wqkv[:, c, 2 * HID:3 * HID], start=c == 0, stop=c == CC - 1)
                        ins.then_inc(v_ps, 1)

                    if b is not None:
                        for i in range(VUNITS // 2):
                            values(i)
                        pe.wait_ge(k_loaded, 16 * 3)
                        pe.wait_ge(q_loaded, 16 * 3)
                        for u in range(PUNITS):
                            th, j = divmod(u, PAIRS)
                            t, h = divmod(th, HEADS)
                            if u >= 3:
                                pe.wait_ge(mx_read, u - 2)
                            for i in range(2):
                                cols = slice((2 * j + i) * NC, (2 * j + i + 1) * NC)
                                ins = nc.tensor.matmul(WIDE[u % 3][:, i * NC:(i + 1) * NC],
                                                       qn[0:3 * DH, h, t * P:(t + 1) * P], kst[0:3 * DH, h, cols],
                                                       start=True, stop=True)
                            ins.then_inc(mx_full, 1)
                            if u % 8 == 7 and u // 8 < VUNITS // 2:
                                values(VUNITS // 2 + u // 8)
                        for h in range(HEADS):
                            pe_neg(pe, h, PUNITS)

                @block.scalar
                def _(act):
                    if fb is not None:
                        act_root(act, 1)
                        act.wait_ge(aff_ready, 1)
                    for i in range(max(VUNITS, CHUNKS)):
                        if b is not None:
                            act.wait_ge(v_ps, i + 1)
                            nc.scalar.activation(vsb[:, 4 * i:4 * i + 4, :].rearrange("p j c -> p (j c)"),
                                                 VB[i % 2], ACT.Copy).then_inc(v_sb, 1)
                        if fb is not None:
                            finish_act(act, i)

                @block.vector
                def _(dve):
                    link = linker(dve)
                    if fb is not None:
                        dve_moments(link, st)
                        dve_group_var(dve, link, 1)
                        dve_rsqrt(dve, link, sm[:, 6, :], 1)
                        dve_affine(link, aff, sm[:, 6, :], v_gnw, v_gnb, aff_ready)
                    if b is not None:
                        for u in range(PUNITS):
                            dve.wait_ge(mx_full, u + 1)
                            nc.vector.reduce_max(mx[:, u // PAIRS, u % PAIRS:u % PAIRS + 1], WIDE[u % 3], AX.X)\
                                .then_inc(mx_read, 1)
                            if fb is not None and u % 8 == 7:
                                finish_dve(dve, u // 8)
                        dve_neg(dve, link, PUNITS, PAIRS)
                        for h in range(HEADS):
                            dve_neg_rows(dve, h, PUNITS)
                        dve_take_q(dve, PUNITS)
                    else:
                        for n in range(CHUNKS):
                            finish_dve(dve, n)
            clear()

        fbufs = [t.rearrange("p (a c n) -> p a c n", a=2, c=CC) for t in pflat[0:2]]

        def finish_loads(sp, b):
            def load(n):
                if n >= 2:
                    sp.wait_ge(stored[n % 2], 16 * (n // 2))
                cols = slice(n * NC, (n + 1) * NC)
                sp.dma_start(fbufs[n % 2][:, 0, :, :], ys[:, :, cols]).then_inc(in_loaded[n % 2], 16)
                sp.dma_start(fbufs[n % 2][:, 1, :, :], x1s[b, :, :, cols]).then_inc(in_loaded[n % 2], 16)
            load(0)
            for n in range(CHUNKS):
                if n + 1 < CHUNKS:
                    load(n + 1)
                sp.wait_ge(out_ready[n % 2], CC * (n // 2 + 1))
                sp.dma_start(ov[b, :, :, n * NC:(n + 1) * NC], fbufs[n % 2][:, 0, :, :]).then_inc(stored[n % 2], 16)
            for i in range(2):
                sp.wait_ge(stored[i], 16 * CHUNKS // 2)

        def finish_act(act, n):
            act.wait_ge(in_loaded[n % 2], 32 * (n // 2 + 1))
            for c in range(CC):
                nc.scalar.activation(fbufs[n % 2][:, 1, c, :], fbufs[n % 2][:, 1, c, :], ACT.Identity,
                                     bias=aff[:, 1, c:c + 1]).then_inc(norm_act, 1)

        def finish_dve(dve, n):
            dve.wait_ge(norm_act, CC * (n + 1))
            for c in range(CC):
                y = fbufs[n % 2][:, 0, c, :]
                nc.vector.scalar_tensor_tensor(y, y, aff[:, 0, c:c + 1], fbufs[n % 2][:, 1, c, :],
                                               ALU.mult, ALU.add).then_inc(out_ready[n % 2], 1)

        def chunk(b, ic, attn, nxt, conv):
            with nc.Block() as block:
                @block.sync
                def _(sp):
                    if nxt:
                        load_q(sp, ic + 1)
                    if attn:
                        sp.dma_start(xr[:, :, :], xv[b, :, :, bass.ds(ic * NC, NC)]).then_inc(loaded, 16)
                    if conv:
                        for s in range(SUBS):
                            sp.wait_ge(y_ready, CC * (s + 1))
                            sp.dma_start(ys[:, :, bass.ds(ic * NC + s * ST * P, ST * P)], yc[s][:, :, :])\
                                .then_inc(stored[1], 16)
                    if attn:
                        sp.wait_ge(x1_ready, CC)
                        sp.dma_start(x1s[b, :, :, bass.ds(ic * NC, NC)], xr[:, :, :]).then_inc(stored[0], 16)
                        sp.wait_ge(stored[0], 16)
                    if nxt:
                        sp.wait_ge(q_loaded, 16 * 3)
                    if conv:
                        sp.wait_ge(stored[1], 16 * SUBS)

                @block.gpsimd
                def _(pool):
                    if conv:
                        nc.gpsimd.tensor_copy(idxc[:, :], widx[:, :, :].rearrange("p t k -> p (t k)")
                                              [:, bass.ds(ic * CT * TAPS, CT * TAPS)]).then_inc(idx_ready, 1)
                        pool.wait_ge(idx_ready, 1)

                    def gather(s):
                        for i in range(ST):
                            u = s * ST + i
                            col = (s // TAPS * ST + i) * TAPS + s % TAPS
                            if u >= NCORN:
                                pool.wait_ge(blended, u - NCORN + 1)
                            nc.gpsimd.indirect_dma_start(
                                corners[u % NCORN][:, :], None, tab,
                                bass.IndirectOffsetOnAxis(ap=idxc[:, col:col + 1].bitcast(U32), axis=0))\
                                .then_inc(gathered[u % NCORN], 16)
                    ahead = NCORN // ST
                    if conv:
                        for s in range(ahead):
                            gather(s)
                    for jt in range(JT):
                        g, r = divmod(jt, SUMG)
                        if attn and r:
                            n = g * (SUMG - 1) + r - 1
                            pool.wait_ge(exp_done, HEADS * (jt + 1))
                            if r == 1 and g >= 2:
                                pool.wait_ge(sum_used, g - 1)
                            if r > 1:
                                pool.wait_ge(p_added, n)
                            left = probs[(jt - 1) % RING] if r == 1 else psums[g % 2]
                            nc.gpsimd.tensor_tensor(psums[g % 2], left, probs[jt % RING], ALU.add).then_inc(p_added, 1)
                        s = step_of(jt) if conv else None
                        if s is not None and s + ahead < STEPS:
                            gather(s + ahead)
                    if conv:
                        for i in range(NCORN):
                            pool.wait_ge(gathered[i], 16 * (ST * STEPS // NCORN))

                @block.scalar
                def _(act):
                    if conv:
                        act.wait_ge(w_ready, 1)

                    def first(s):
                        if s >= 2:
                            act.wait_ge(vt_full, s - 1)
                        for i in range(ST):
                            u = s * ST + i
                            col = (s // TAPS * ST + i) * TAPS + s % TAPS
                            act.wait_ge(gathered[u % NCORN], 16 * (u // NCORN + 1))
                            nc.scalar.activation(vpix[s % 2][:, i, :], corners[u % NCORN][:, 0:C], ACT.Copy,
                                                 scale=wcur[:, 0, col:col + 1]).then_inc(first_corner, 1)

                    def evacuate(s):
                        act.wait_ge(vt_full, s + 1)
                        if s >= 2:
                            act.wait_ge(conv_done, s - 1)
                        nc.scalar.activation(vT[s % 2][:, :, :].rearrange("p c n -> p (c n)"), VT,
                                             ACT.Copy).then_inc(vt_sb, 1)

                    def finish(sub):
                        act.wait_ge(conv_done, TAPS * (sub + 1))
                        for o in range(CC):
                            nc.scalar.activation(yc[sub][:, o, :], Y[:, o * ST * P:(o + 1) * ST * P], ACT.Identity,
                                                 bias=v_bconv[:, o:o + 1]).then_inc(y_ready, 1)
                    if conv:
                        first(0)
                    for jt in range(JT):
                        if attn:
                            for h in range(HEADS):
                                u = jt * HEADS + h
                                if h == 0 and jt >= RING:
                                    g, r = divmod(jt - RING, SUMG)
                                    act.wait_ge(p_used, jt - RING + 1)
                                    act.wait_ge(p_added, g * (SUMG - 1) + max(1, r))
                                act.wait_ge(s_full, u + 1)
                                nc.scalar.activation(probs[jt % RING][:, h, :], S[u % 2], ACT.Exp,
                                                     scale=escale[:, :]).then_inc(exp_done, 1)
                        s = step_of(jt) if conv else None
                        if s is not None:
                            if s + 1 < STEPS:
                                first(s + 1)
                            evacuate(s)
                            if s == TAPS:
                                finish(0)
                    if conv:
                        finish(1)

                @block.vector
                def _(dve):
                    link = linker(dve)

                    if conv:
                        nc.vector.tensor_copy(wcur[:, :, :], wall[:, :, :, :].rearrange("p q t k -> p q (t k)")
                                              [:, :, bass.ds(ic * CT * TAPS, CT * TAPS)]).then_inc(w_ready, 1)
                        dve.wait_ge(w_ready, 1)

                    def y_stats(sub):
                        dve.wait_ge(y_ready, CC * (sub + 1))
                        for o in range(CC):
                            nc.vector.bn_stats(st[:, o, bass.ds(ic * SUBS + sub, 1), :].rearrange("p a s -> p (a s)"),
                                               yc[sub][:, o, :])

                    def blend(s):
                        for q in range(1, 4):
                            for i in range(ST):
                                u = s * ST + i
                                col = (s // TAPS * ST + i) * TAPS + s % TAPS
                                v = vpix[s % 2][:, i, :]
                                if q == 1:
                                    dve.wait_ge(gathered[u % NCORN], 16 * (u // NCORN + 1))
                                    dve.wait_ge(first_corner, u + 1)
                                else:
                                    dve.wait_ge(blend_chain, (s * 2 + q - 2) * ST + i + 1)
                                nc.vector.scalar_tensor_tensor(v, corners[u % NCORN][:, q * C:(q + 1) * C],
                                                               wcur[:, q, col:col + 1], v, ALU.mult, ALU.add)\
                                    .then_inc(blended if q == 3 else blend_chain, 1)

                    for jt in range(JT):
                        s = step_of(jt) if conv else None
                        if s is not None:
                            blend(s)
                            if s == TAPS + 1:
                                y_stats(0)
                        if nxt and jt >= MAX_FROM:
                            u0 = (jt - MAX_FROM) * MAX_PER_JT
                            for u in range(u0, min(u0 + MAX_PER_JT, MAX_UNITS)):
                                dve_max(dve, u)
                            if jt == NEG_AT - 1:
                                dve_neg(dve, link, MAX_UNITS, CHUNKS)
                            if jt >= NEG_AT:
                                dve_neg_rows(dve, jt - NEG_AT, MAX_UNITS)
                    if conv:
                        y_stats(1)
                    if attn:
                        dve.wait_ge(sum_used, JT // SUMG)
                        dve.wait_ge(p_used, JT)
                        nc.vector.reciprocal(rsum[:, :], SUM).then_inc(attn_ready, 1)
                        dve.wait_ge(attn_ready, 1)
                        nc.vector.tensor_tensor(an[:, :], PV, rsum[:, :], ALU.mult).then_inc(attn_ready, 1)
                        if nxt:
                            dve_take_q(dve, MAX_UNITS)
                        dve.wait_ge(loaded, 16)
                        for o in range(CC):
                            dve.wait_ge(proj_full, o + 1)
                            nc.vector.scalar_tensor_tensor(xr[:, o, :], S[o], v_bout[:, o:o + 1], xr[:, o, :],
                                                           ALU.add, ALU.add).then_inc(x1_ready, 1)
                        for o in range(CC):
                            dve.wait_ge(x1_ready, o + 1)
                            nc.vector.bn_stats(st1[:, o, bass.ds(ic, 1), :].rearrange("p a s -> p (a s)"), xr[:, o, :])

                @block.tensor
                def _(pe):
                    def turn(s):
                        pe.wait_ge(blended, ST * (s + 1))
                        if s:
                            pe.wait_ge(vt_sb, s)
                        for c in range(CC):
                            for i in range(ST):
                                ins = nc.tensor.transpose(VT[:, (c * ST + i) * P:(c * ST + i + 1) * P],
                                                          vpix[s % 2][:, i, c * P:(c + 1) * P], ident[:, :])
                        ins.then_inc(vt_full, 1)

                    def convolve(s):
                        sub, tap = divmod(s, TAPS)
                        pe.wait_ge(vt_sb, s + 1)
                        if tap == 0 and sub:
                            pe.wait_ge(y_ready, CC * sub)
                        for c in range(CC):
                            for o in range(CC):
                                ins = nc.tensor.matmul(Y[:, o * ST * P:(o + 1) * ST * P],
                                                       wc[:, c * TAPS + tap, o * P:(o + 1) * P], vT[s % 2][:, c, :],
                                                       start=tap == 0 and c == 0 and o == 0,
                                                       stop=tap == TAPS - 1 and c == CC - 1, skip_group_check=True)
                        ins.then_inc(conv_done, 1)

                    def scores(jt, h):
                        u = jt * HEADS + h
                        if u >= 2:
                            pe.wait_ge(exp_done, u - 1)
                        nc.tensor.matmul(S[u % 2], kst[0:ROWS, h, jt * P:(jt + 1) * P], qc[0:ROWS, h, :], start=True,
                                         stop=True).then_inc(s_full, 1)

                    def weigh(jt):
                        pe.wait_ge(exp_done, HEADS * (jt + 1))
                        for h in range(HEADS):
                            band = slice(h * DH, (h + 1) * DH)
                            ins = nc.tensor.matmul(PV[band, :], vsb[:, jt, band], probs[jt % RING][:, h, :],
                                                   start=jt == 0, stop=jt == JT - 1, tile_position=(0, h * DH),
                                                   skip_group_check=True)
                        ins.then_inc(p_used, 1)

                    def add_up(g):
                        pe.wait_ge(p_added, (SUMG - 1) * (g + 1))
                        for h in range(HEADS):
                            ins = nc.tensor.matmul(SUM[h * DH:(h + 1) * DH, :], ones[:, :], psums[g % 2][:, h, :],
                                                   start=g == 0, stop=g == JT // SUMG - 1,
                                                   tile_position=(0, h * DH), skip_group_check=True)
                        ins.then_inc(sum_used, 1)

                    if nxt:
                        pe.wait_ge(q_loaded, 16 * 3)
                    for jt in range(JT):
                        units = []
                        if nxt and jt >= MAX_FROM:
                            u0 = (jt - MAX_FROM) * MAX_PER_JT
                            units = list(range(u0, min(u0 + MAX_PER_JT, MAX_UNITS)))

                        def maxima(m=1):
                            for _ in range(m):
                                if units:
                                    pe_max(pe, units.pop(0))
                        s = step_of(jt) if conv else None
                        if attn:
                            scores(jt, 0)
                            scores(jt, 1)
                        maxima()
                        if attn and jt:
                            weigh(jt - 1)
                        maxima()
                        if attn:
                            scores(jt, 2)
                            scores(jt, 3)
                        maxima()
                        if s is not None:
                            turn(s)
                        if attn and jt > SUMG and (jt - 1) % SUMG == 0:
                            add_up((jt - 1) // SUMG - 1)
                        maxima()
                        if s:
                            convolve(s - 1)
                        maxima(MAX_PER_JT)
                        if nxt and jt >= NEG_AT:
                            pe_neg(pe, jt - NEG_AT, MAX_UNITS)
                    if conv:
                        convolve(STEPS - 1)
                    if attn:
                        weigh(JT - 1)
                        add_up(JT // SUMG - 1)
                        pe.wait_ge(attn_ready, 2)
                        for o in range(CC):
                            nc.tensor.matmul(S[o], wout[:, o * P:(o + 1) * P], an[:, :], start=True,
                                             stop=True).then_inc(proj_full, 1)
            clear()

        def between(pb, b):
            pre = 1 if pb is not None else 0

            with nc.Block() as block:
                @block.sync
                def _(sp):
                    if pb is not None:
                        for c in range(CC):
                            sp.dma_start(xs[:, c, :], x1s[pb, :, c, :]).then_inc(loaded, 16)
                        sp.wait_ge(norm_act, 1)
                        sp.wait_ge(norm_dve, 1)
                    if b is not None:
                        for c in range(CC):
                            sp.dma_start(xs[:, c, :], xv[b, :, c, :]).then_inc(x_loaded, 16)
                    if pb is not None:
                        for g, m in enumerate(PGROUPS):
                            sp.wait_ge(px_act, g + 1)
                            sp.wait_ge(px_dve, min(g + 1, PTILES // 4))
                            for q in range(4):
                                first = LEAD + 4 * g * P - (q // 2 * WP + q % 2)
                                dst = tab[first:first + m * P, q * C:(q + 1) * C].rearrange("(t p) c -> p t c", p=P)
                                src = corners[g % 4][:, 0:m * C].rearrange("p (t c) -> p t c", t=m)
                                sp.dma_start(dst, src).then_inc(px_stored[g % 4], 16)
                    if b is not None:
                        for i in range(2 * CHUNKS):
                            which, n = 1 - i // CHUNKS, i % CHUNKS
                            sp.wait_ge(qk_lo, i + 1)
                            sp.dma_start(qkp[which, :, :, n * NC:(n + 1) * NC].rearrange("r p n -> p r n"),
                                         parts[i % 4][:, :, :]).then_inc(stored[i % 4], 16)
                        for i in range(4):
                            sp.wait_ge(stored[i], 16 * 2 * CHUNKS // 4)
                        sp.wait_ge(x_loaded, 16 * CC)
                    if pb is not None:
                        for i in range(4):
                            sp.wait_ge(px_stored[i], 64 * len(PGROUPS[i::4]))

                @block.gpsimd
                def _(pool):
                    if pb is not None:
                        for c in range(CC):
                            nc.gpsimd.memset(h1[:, c, 0, :], 0.0)
                            nc.gpsimd.memset(h1[:, c, HP - 1, :], 0.0)
                            nc.gpsimd.memset(h1[:, c, 1:HP - 1, 0:1], 0.0)
                            nc.gpsimd.memset(h1[:, c, 1:HP - 1, WP - 1:WP], 0.0).then_inc(ring_zero, 1)
                    if b is not None:
                        pool.wait_ge(amax_ready, 1)
                        nc.gpsimd.partition_all_reduce(pow2[:, :], amax2[:, :], P, RMAX).then_inc(amax_all, 1)

                @block.scalar
                def _(act):
                    if pb is not None:
                        act_root(act, 1)
                        act.wait_ge(aff_ready, 1)
                        act.wait_ge(loaded, 16 * CC)
                        nc.scalar.activation(h1[:, 0, 1:H + 1, 1:W + 1],
                                             xs[:, 0, :].rearrange("p (y x) -> p y x", x=W), ACT.Identity,
                                             bias=aff[:, 1, 0:1], scale=aff[:, 0, 0:1]).then_inc(norm_act, 1)
                        for r in range(2):
                            act.wait_ge(off_full, r + 1)
                            nc.scalar.activation(pflat[0][:, r * NC:(r + 1) * NC], S[r], ACT.Identity,
                                                 bias=v_boff[:, :]).then_inc(off_sb, 1)
                    if b is not None:
                        act_root(act, pre + 1)
                        act_root(act, pre + 2)
                        act.wait_ge(aff_ready, pre + 1)
                        nc.scalar.activation(xs[:, 0, :], xs[:, 0, :], ACT.Identity, bias=affx[:, 1, 0:1],
                                             scale=affx[:, 0, 0:1]).then_inc(norm_act, 1)
                    if pb is not None:
                        for j in range(0, PTILES // 2, 2):
                            if j >= 8:
                                act.wait_ge(px_stored[j // 2 % 4], 64 * (j // 8))
                            act.wait_ge(px_full, j + 1)
                            nc.scalar.activation(corners[j // 2 % 4][:, 0:NC], banks[4 + j % 4], ACT.Copy)\
                                .then_inc(px_act, 1)
                    if b is not None:
                        for i in range(2 * CHUNKS):
                            which, n = 1 - i // CHUNKS, i % CHUNKS
                            act.wait_ge(qk_ps, i + 1)
                            nc.scalar.activation(qkf[:, which, n * NC:(n + 1) * NC], banks[i % 4], ACT.Copy)\
                                .then_inc(qk_sb, 1)
                        act.wait_ge(lift_ready, 1)
                        for i in range(2 * CHUNKS):
                            which, n = 1 - i // CHUNKS, i % CHUNKS
                            if i >= 4:
                                act.wait_ge(stored[i % 4], 16 * (i // 4))
                            act.wait_ge(qk_sb, i + 1)
                            nc.scalar.activation(parts[i % 4][:, 0, :], qkf[:, which, n * NC:(n + 1) * NC], ACT.Copy,
                                                 scale=lift[:, which:which + 1]).then_inc(qk_hi, 1)

                @block.tensor
                def _(pe):
                    if pb is not None:
                        pe_group_means(pe, 1)
                        pe.wait_ge(norm_act, 1)
                        pe.wait_ge(norm_dve, 1)
                        pe.wait_ge(ring_zero, CC)
                        for r in range(2):
                            for c in range(CC):
                                for tap in range(TAPS):
                                    ky, kx = divmod(tap, K)
                                    for t in range(4):
                                        y0 = 8 * (4 * r + t) + ky
                                        ins = nc.tensor.matmul(
                                            S[r][DH * t:DH * (t + 1), :], woff[:, c * TAPS + tap, :],
                                            h1[:, c, y0:y0 + 8, kx:kx + W], start=c == 0 and tap == 0,
                                            stop=c == CC - 1 and tap == TAPS - 1, tile_position=(0, DH * t),
                                            skip_group_check=True)
                            ins.then_inc(off_full, 1)
                    if b is not None:
                        pe_group_means(pe, pre + 1)
                    if pb is not None:
                        for r in range(2):
                            pe.wait_ge(off_sb, r + 1)
                            for q in range(4):
                                ins = nc.tensor.transpose(MX[r][:, q * P:(q + 1) * P],
                                                          pflat[0][:, r * NC + q * P:r * NC + (q + 1) * P], ident[:, :])
                            ins.then_inc(offT_full, 1)
                    if b is not None:
                        pe.wait_ge(mom_ready, pre + 2)
                        nc.tensor.matmul(VT[:, 4 * CC:5 * CC], allmean[:, :], sm[:, 9, :], start=True, stop=True)\
                            .then_inc(grp_ready, 1)
                        pe.wait_ge(root_in, pre + 2)
                    if pb is not None:
                        for j in range(PTILES // 2):
                            if j >= 4:
                                pe.wait_ge(px_dve if j % 2 else px_act, (j - 4) // 2 + 1)
                            for i in range(2):
                                for c in range(CC):
                                    e0 = (2 * j + i) * P
                                    ins = nc.tensor.transpose(
                                        banks[4 + j % 4][:, (i * CC + c) * P:(i * CC + c + 1) * P],
                                        h1flat[:, c, e0:e0 + P], ident[:, :])
                            ins.then_inc(px_full, 1)
                    if b is not None:
                        pe.wait_ge(norm_act, pre + 1)
                        pe.wait_ge(norm_dve, pre + 1)
                        if pb is not None:
                            pe.wait_ge(off_sb, 2)
                            pe.wait_ge(offT_read, 2)
                        for i in range(2 * CHUNKS):
                            which, n = 1 - i // CHUNKS, i % CHUNKS
                            if i >= 4:
                                pe.wait_ge(qk_sb, i - 3)
                            for c in range(CC):
                                ins = nc.tensor.matmul(banks[i % 4], wqkv[:, c, which * HID:(which + 1) * HID],
                                                       xs[:, c, n * NC:(n + 1) * NC], start=c == 0, stop=c == CC - 1)
                            ins.then_inc(qk_ps, 1)

                @block.vector
                def _(dve):
                    link = linker(dve)
                    if pb is not None:
                        dve_moments(link, st1)
                        dve_group_var(dve, link, 1)
                        dve_rsqrt(dve, link, aff[:, 0, :], 1)
                        dve_affine(link, aff, None, None, None, aff_ready)
                        dve.wait_ge(aff_ready, 1)
                        dve.wait_ge(loaded, 16 * CC)
                        nc.vector.tensor_scalar(h1[:, 1, 1:H + 1, 1:W + 1],
                                                xs[:, 1, :].rearrange("p (y x) -> p y x", x=W),
                                                aff[:, 0, 1:2], aff[:, 1, 1:2], ALU.mult, ALU.add).then_inc(norm_dve, 1)
                    if b is not None:
                        dve.wait_ge(x_loaded, 16 * CC)
                        for c in range(CC):
                            for n in range(CHUNKS):
                                ins = nc.vector.bn_stats(st1[:, c, n, :], xs[:, c, n * NC:(n + 1) * NC])
                        link(ins)
                        dve_moments(link, st1)
                        dve_group_var(dve, link, pre + 1)
                        dve_rsqrt(dve, link, sm[:, 6, :], pre + 1)
                        link(nc.vector.tensor_tensor(sm[:, 8, :], sm[:, 6, :], sm[:, 6, :], ALU.mult))
                        nc.vector.tensor_tensor(sm[:, 9, :], sm[:, 8, :], sm[:, 5, :], ALU.mult).then_inc(mom_ready, 1)
                        dve.wait_ge(grp_ready, pre + 2)
                        link(nc.vector.reduce_sum(sm[:, 10, 0:1], VT[:, 4 * CC:5 * CC], AX.X))
                        link(nc.vector.tensor_scalar(sm[:, 0, 0:1], sm[:, 10, 0:1], EPS, None, ALU.add))
                        nc.vector.tensor_copy(sm[:, 0, 1:2], sm[:, 0, 0:1]).then_inc(root_in, 1)
                        dve_rsqrt(dve, link, sm[:, 8, :], pre + 2)
                        link(nc.vector.tensor_tensor(sm[:, 9, :], sm[:, 6, :], sm[:, 8, :], ALU.mult))
                        dve_affine(link, affx, sm[:, 9, :], v_gamma, v_beta, aff_ready)
                        dve.wait_ge(aff_ready, pre + 1)
                        nc.vector.tensor_scalar(xs[:, 1, :], xs[:, 1, :], affx[:, 0, 1:2], affx[:, 1, 1:2],
                                                ALU.mult, ALU.add).then_inc(norm_dve, 1)
                    if pb is not None:
                        for r in range(2):
                            dve.wait_ge(offT_full, r + 1)
                            nc.vector.tensor_copy(
                                offall[:, 16 * r:16 * (r + 1), :].rearrange("p (t q) o -> p q t o", t=4),
                                MX[r].rearrange("p (q t o) -> p q t o", q=4, t=4)[:, :, :, 0:OFFS])\
                                .then_inc(offT_read, 1)
                        for j in range(1, PTILES // 2, 2):
                            if j >= 8:
                                dve.wait_ge(px_stored[j // 2 % 4], 64 * (j // 8))
                            dve.wait_ge(px_full, j + 1)
                            nc.vector.tensor_copy(corners[j // 2 % 4][:, NC:2 * NC], banks[4 + j % 4])\
                                .then_inc(px_dve, 1)
                    if b is not None:
                        for i in range(2 * CHUNKS):
                            which, n = 1 - i // CHUNKS, i % CHUNKS
                            dve.wait_ge(qk_sb, i + 1)
                            nc.vector.reduce_max(amax[:, which, n:n + 1], qkf[:, which, n * NC:(n + 1) * NC], AX.X,
                                                 apply_absolute_value=True).then_inc(amax_read, 1)
                        dve.wait_ge(amax_read, 2 * CHUNKS)
                        link(nc.vector.reduce_max(amax2[:, :], amax[:, :, :], AX.X))
                        nc.vector.tensor_scalar(amax2[:, :], amax2[:, :], 1e-30, None, ALU.max).then_inc(amax_ready, 1)
                        dve.wait_ge(amax_all, 1)
                        link(nc.vector.tensor_scalar(pow2[:, :].bitcast(I32), pow2[:, :].bitcast(I32), 0x7F800000, None,
                                                     ALU.bitwise_and))
                        link(nc.vector.reciprocal(lift[:, :], pow2[:, :]))
                        nc.vector.tensor_scalar(lift[:, :], lift[:, :], LIFT, None, ALU.mult).then_inc(lift_ready, 1)
                        link(nc.vector.tensor_scalar(escale[:, :], pow2[:, 0:1], SCALE / LIFT / LIFT, None, ALU.mult))
                        link(nc.vector.tensor_tensor(escale[:, :], escale[:, :], pow2[:, 1:2], ALU.mult))
                        for i in range(2 * CHUNKS):
                            which, n = 1 - i // CHUNKS, i % CHUNKS
                            dve.wait_ge(qk_hi, i + 1)
                            nc.vector.scalar_tensor_tensor(parts[i % 4][:, 1, :], qkf[:, which, n * NC:(n + 1) * NC],
                                                           lift[:, which:which + 1], parts[i % 4][:, 0, :],
                                                           ALU.mult, ALU.subtract).then_inc(qk_lo, 1)
                    if pb is not None:
                        dve.wait_ge(offT_read, 2)
                        sample_points(link)
            clear()

        def sample_points(link):
            n = TILES * OFFS
            pos = offall[:, :, :].rearrange("p t o -> p (t o)")
            t0, t1, t2 = (pflat[1][:, i * n:(i + 1) * n] for i in range(3))
            link(nc.vector.tensor_tensor(pos, pos, base[:, :, :].rearrange("p t o -> p (t o)"), ALU.add))
            link(nc.vector.tensor_scalar(pos, pos, 0.0, float(HP - 1), ALU.max, ALU.min))
            whole = t0.bitcast(I32)
            link(nc.vector.tensor_copy(whole, pos))
            link(nc.vector.tensor_copy(t1, whole))
            link(nc.vector.tensor_tensor(t2, t1, pos, ALU.is_gt))
            link(nc.vector.tensor_tensor(t1, t1, t2, ALU.subtract))
            link(nc.vector.tensor_tensor(pos, pos, t1, ALU.subtract))
            link(nc.vector.tensor_scalar(t2, pos, -1.0, 1.0, ALU.mult, ALU.add))
            fy, fx = offall[:, :, 0:TAPS], offall[:, :, TAPS:OFFS]
            far = t2.rearrange("p (t o) -> p t o", o=OFFS)
            gy, gx = far[:, :, 0:TAPS], far[:, :, TAPS:OFFS]
            low = t1.rearrange("p (t o) -> p t o", o=OFFS)
            for q, (wy, wx) in enumerate(((gy, gx), (gy, fx), (fy, gx), (fy, fx))):
                nc.vector.tensor_tensor(wall[:, q, :, :], wy, wx, ALU.mult)
            t0v = t0.rearrange("p (t o) -> p t o", o=OFFS)[:, :, 0:TAPS]
            link(nc.vector.scalar_tensor_tensor(t0v, low[:, :, 0:TAPS], float(WP), low[:, :, TAPS:OFFS],
                                                ALU.mult, ALU.add))
            link(nc.vector.tensor_scalar(t0v, t0v, float(LEAD), None, ALU.add))
            link(nc.vector.tensor_copy(widx[:, :, :], t0v))

        def attend(b, conv):
            with nc.Fori(0, CHUNKS - 1) as ic:
                chunk(b, ic, True, True, conv)
            chunk(b, CHUNKS - 1, True, False, conv)

        between(None, 0)
        first_max(0, None)
        attend(0, False)
        between(0, 1)
        first_max(1, None)
        attend(1, True)
        with nc.Fori(2, B) as b:
            between(b - 1, b)
            first_max(b, b - 2)
            attend(b, True)
        between(B - 1, None)
        first_max(None, B - 2)
        with nc.Fori(0, CHUNKS) as ic:
            chunk(None, ic, False, False, True)
        first_max(None, B - 1)


def kernel(**inputs):
    import numpy as _np
    import concourse.bacc as _bacc
    from concourse import mybir as _mybir
    from concourse.bass_utils import run_bass_kernel_spmd as _run

    a = {k: _np.asarray(v) for k, v in inputs.items()}

    def halves(v):
        return v.reshape(CC, P).T

    px = _np.arange(N).reshape(TILES, P)
    base = _np.zeros((P, TILES, OFFS), _np.float32)
    for k in range(TAPS):
        base[:, :, k] = (px // W + k // K).T
        base[:, :, TAPS + k] = (px % W + k % K).T
    arrays = {
        "x": a["x"],
        "gamma": halves(a["L0_conv_gamma"]),
        "beta": halves(a["L0_conv_beta"]),
        "wqkvT": a["L0_conv_w_qkv"].T.reshape(CC, P, 3 * HID).transpose(1, 0, 2),
        "woutT": a["L0_conv_w_out"].T,
        "bout": halves(a["L0_conv_b_out"]),
        "woffT": a["L1_conv_w_off"].reshape(OFFS, CC, P, TAPS).transpose(2, 1, 3, 0).reshape(P, CC * TAPS, OFFS),
        "boff": a["L1_conv_b_off"].reshape(OFFS, 1),
        "wcT": a["L1_conv_w"].reshape(C, CC, P, TAPS).transpose(2, 1, 3, 0).reshape(P, CC * TAPS, C),
        "bconv": halves(a["L1_conv_b"]),
        "gnw": halves(a["L1_conv_gn_w"]),
        "gnb": halves(a["L1_conv_gn_b"]),
        "ident": _np.eye(P, dtype=_np.float32),
        "gmean": (_np.kron(_np.eye(P // GROUP), _np.ones((GROUP, GROUP))) / GROUP).astype(_np.float32),
        "allmean": _np.full((P, P), 1.0 / C, _np.float32),
        "base": base,
    }
    arrays = {k: _np.ascontiguousarray(v) for k, v in arrays.items()}
    nc = _bacc.Bacc("TRN2", target_bir_lowering=False, num_devices=1)
    args = [nc.dram_tensor(f"in_{k}", v.shape, _mybir.dt.float32, kind="ExternalInput").ap() for k, v in arrays.items()]
    out = nc.dram_tensor("out_0", (B, C, H, W), _mybir.dt.float32, kind="ExternalOutput").ap()
    build(nc, *args, out)
    r = _run(nc, [{f"in_{k}": v for k, v in arrays.items()}], core_ids=[0])
    return r.results[0]["out_0"]
```

```python
import concourse.bass as bass
from concourse import mybir
from contextlib import ExitStack

F32 = mybir.dt.float32
F16 = mybir.dt.float16
I32 = mybir.dt.int32
U32 = mybir.dt.uint32
RMAX = bass.bass_isa.ReduceOp.max
ACT = mybir.ActivationFunctionType
ALU = mybir.AluOpType
AX = mybir.AxisListType

B, C, H, W = 4, 256, 64, 64
P = 128
CC = C // P
N = H * W
NC = 512
CHUNKS = N // NC
HEADS, DH = 4, 32
HID = HEADS * DH
SCALE = DH ** -0.5
JT = N // P
K, TAPS = 3, 9
HP, WP = H + 2, W + 2
EPS = 1e-5
GROUP = C // 32
TILES = N // P
LEAD = WP + 1
PTILES = HP * WP // P
PGROUPS = [4] * (PTILES // 4) + [PTILES % 4]
OFFS = 2 * TAPS
CT = NC // P
SUBS = 2
STEPS = SUBS * TAPS
ST = CT // SUBS
MAX_UNITS = CT * HEADS * CHUNKS
LIFT = 2.0 ** 11
ONE = 2.0 ** 15
ROWS = 3 * DH + 3
RING = 3
SUMG = 2
FBUFS = 4
NCORN = 6
NEG_AT = JT - 2


SLOTS = STEPS + 2
FROM = 2
SLOT_OF = {FROM + v * (JT - 1 - FROM) // SLOTS: v for v in range(SLOTS)}


def max_plan(conv):
    plan, left = [0] * JT, MAX_UNITS
    for jt in range(FROM, NEG_AT):
        plan[jt] = min(left, (4 if jt in SLOT_OF else 6) if conv else 5)
        left -= plan[jt]
    assert left == 0
    return plan


def build(nc, x, gamma, beta, wqkvT, woutT, bout, woffT, boff, wcT, bconv, gnw, gnb,
          ident_c, gmean_c, all_c, base_c, out):
    xv = x.rearrange("b (cc p) h w -> b p cc (h w)", p=P)
    ov = out.rearrange("b (cc p) h w -> b p cc (h w)", p=P)
    qkp = nc.dram_tensor("qk_parts", (2, 2, HID, N), F16).ap()
    x1s = nc.dram_tensor("x1_scratch", (B, P, CC, N), F32).ap()
    ys = nc.dram_tensor("y_scratch", (P, CC, N), F32).ap()
    tab = nc.dram_tensor("corner_table", (LEAD + HP * WP, 4 * C), F32).ap()

    ctx = ExitStack()
    with ctx:
        def sb(name, shape, dt=F32):
            return ctx.enter_context(nc.sbuf_tensor(name, shape, dt))

        ident = sb("ident", [P, P])
        identh = sb("identh", [P, P], F16)
        gmean = sb("gmean", [P, P])
        allmean = sb("allmean", [P, P])
        ones = sb("ones", [P, DH])
        base = sb("base", [P, TILES, OFFS])
        wqkv = sb("wqkv", [P, CC, 3 * HID])
        wout = sb("wout", [P, C])
        woff = sb("woff", [P, CC * TAPS, DH])
        wc = sb("wc", [P, CC * TAPS, C])
        vecs = sb("vecs", [P, 6, CC])
        v_gamma, v_beta, v_bout, v_bconv, v_gnw, v_gnb = (vecs[:, i, :] for i in range(6))
        v_boff = sb("v_boff", [P, 1])

        kk = sb("kk", [P, HP * WP * CC * 2], F16)
        kst = kk[:, 0:HEADS * N].rearrange("p (h j) -> p h j", h=HEADS)
        qkf = kk[:, 0:2 * 2 * N].bitcast(F32).rearrange("p (w n) -> p w n", w=2)
        h1 = kk[:, :].bitcast(F32).rearrange("p (cc y x) -> p cc y x", cc=CC, x=WP)
        h1flat = h1.rearrange("p cc y x -> p cc (y x)")
        wide = sb("wide", [P, CC * N])
        xs = wide[:, :].rearrange("p (cc n) -> p cc n", cc=CC)
        quarter = [wide[:, i * HEADS * NC:(i + 1) * HEADS * NC] for i in range(4)]

        vsb = sb("vsb", [P, JT, HID])
        qn = sb("qn", [P, HEADS, NC], F16)
        qc = sb("qc", [P, HEADS, NC], F16)
        pflat = [sb(f"probs{i}", [P, HEADS * NC])[:, :] for i in range(2)] + [quarter[0]]
        probs = [t.rearrange("p (h n) -> p h n", h=HEADS) for t in pflat]
        psums = [t.rearrange("p (h n) -> p h n", h=HEADS) for t in quarter[1:3]]
        parts = [sb(f"parts{i}", [P, 2, NC], F16) for i in range(4)]
        amax = sb("amax", [P, 2, CHUNKS])
        amax2 = sb("amax2", [P, 2])
        pow2 = sb("pow2", [P, 2])
        lift = sb("lift", [P, 2])
        escale = sb("escale", [P, 1])
        mx = sb("mx", [P, CT * HEADS, CHUNKS])
        neg = sb("neg", [P, CT * HEADS])
        neg2 = sb("neg2", [P, CT * HEADS])
        negp = sb("negp", [P, CT * HEADS, 3], F16)
        rsum = sb("rsum", [P, NC])
        an = sb("an", [P, NC])
        xr = sb("xr", [P, CC, NC])
        st = sb("st", [P, CC, 2 * CHUNKS, 6])
        st1 = sb("st1", [P, CC, CHUNKS, 6])
        mv = sb("mv", [P, CC, 2])
        mom = sb("mom", [P, 2, CC])
        gm = sb("gm", [P, 2, CC])
        sm = sb("sm", [P, 12, CC])
        aff = sb("aff", [P, 2, CC])
        affx = sb("affx", [P, 2, CC])
        offall = sb("offall", [P, TILES, OFFS])
        widx = sb("widx", [P, TILES, TAPS], I32)
        wall = sb("wall", [P, 4, TILES, TAPS])
        idxc = sb("idxc", [P, CT * TAPS], I32)
        wcur = sb("wcur", [P, 4, CT * TAPS])
        corners = [sb(f"corners{i}", [P, 4 * C]) for i in range(4)]
        corners += [quarter[3][:, i * 4 * C:(i + 1) * 4 * C] for i in range(2)]
        vpix = [sb(f"vpix{i}", [P, ST, C]) for i in range(3)]
        vT = [sb(f"vT{i}", [P, CC, ST * P]) for i in range(2)]
        yc = [sb(f"yc{i}", [P, CC, ST * P]) for i in range(2)]

        ps = ctx.enter_context(nc.psum_tensor("ps", [P, 8, NC], F32))
        banks = [ps[:, i, :] for i in range(8)]
        S, MX = banks[0:2], banks[2:4]
        PV, SUM, VT, Y = banks[4:8]
        WIDE = [ps[:, 2 * i:2 * i + 2, :].rearrange("p b n -> p (b n)") for i in range(3)]
        VB = banks[6:8]

        sems = []

        def sem(name):
            s = ctx.enter_context(nc.semaphore(name))
            sems.append(s)
            return s

        loaded = sem("loaded")
        chain = sem("chain")
        mom_ready, grp_ready = sem("mom_ready"), sem("grp_ready")
        root_in, root_out = sem("root_in"), sem("root_out")
        aff_ready = sem("aff_ready")
        norm_act, norm_dve = sem("norm_act"), sem("norm_dve")
        qk_ps, qk_sb, qk_hi, qk_lo = (sem(n) for n in ("qk_ps", "qk_sb", "qk_hi", "qk_lo"))
        amax_read, amax_ready, amax_all, lift_ready = (
            sem(n) for n in ("amax_read", "amax_ready", "amax_all", "lift_ready"))
        x_loaded, k_loaded, px_stored = sem("x_loaded"), sem("k_loaded"), [sem(f"px_stored{i}") for i in range(4)]
        stored = [sem(f"stored{i}") for i in range(4)]
        v_ps, v_sb = sem("v_ps"), sem("v_sb")
        ones_set = sem("ones_set")
        q_loaded = sem("q_loaded")
        mx_full, mx_read, neg_ready = sem("mx_full"), sem("mx_read"), sem("neg_ready")
        s_full, exp_done, p_used = (sem(n) for n in ("s_full", "exp_done", "p_used"))
        attn_ready, proj_full, x1_ready = sem("attn_ready"), sem("proj_full"), sem("x1_ready")
        idx_ready, w_ready, blend_chain = sem("idx_ready"), sem("w_ready"), sem("blend_chain")
        sum_used, offT_read = sem("sum_used"), sem("offT_read")
        gathered = [sem(f"gathered{i}") for i in range(NCORN)]
        p_added, first_corner = sem("p_added"), sem("first_corner")
        blended, vt_full, vt_sb, conv_done, y_ready = (
            sem(n) for n in ("blended", "vt_full", "vt_sb", "conv_done", "y_ready"))
        ring_zero, off_full, off_sb, offT_full, offT_sb = (
            sem(n) for n in ("ring_zero", "off_full", "off_sb", "offT_full", "offT_sb"))
        px_full, px_act, px_dve = sem("px_full"), sem("px_act"), sem("px_dve")
        in_loaded = [sem(f"in_loaded{i}") for i in range(FBUFS)]
        out_ready = [sem(f"out_ready{i}") for i in range(FBUFS)]

        def clear():
            nc.gpsimd.dma_reset(range(gathered[0].num, gathered[-1].num + 1))
            nc.gpsimd.sem_clear(range(sems[0].num, sems[-1].num + 1))
            nc.all_engine_barrier()

        def linker(dve):
            n = [0]

            def link(ins):
                n[0] += 1
                ins.then_inc(chain, 1)
                dve.wait_ge(chain, n[0])
            return link

        def dve_moments(link, stats):
            for c in range(CC):
                link(nc.vector.bn_aggr(mv[:, c, :], stats[:, c, :, :].rearrange("p a s -> p (a s)")))
            link(nc.vector.tensor_tensor(mom[:, 1, :], mv[:, :, 0], mv[:, :, 0], ALU.mult))
            link(nc.vector.tensor_tensor(mom[:, 1, :], mom[:, 1, :], mv[:, :, 1], ALU.add))
            nc.vector.tensor_copy(mom[:, 0, :], mv[:, :, 0]).then_inc(mom_ready, 1)

        def pe_group_means(pe, n):
            pe.wait_ge(mom_ready, n)
            nc.tensor.matmul(VT[:, 0:2 * CC], gmean[:, :], mom[:, :, :].rearrange("p s c -> p (s c)"),
                             start=True, stop=True).then_inc(grp_ready, 1)

        def act_root(act, n):
            act.wait_ge(root_in, n)
            nc.scalar.activation(sm[:, 1, :], sm[:, 0, :], ACT.Sqrt).then_inc(root_out, 1)

        def dve_rsqrt(dve, link, out_ap, n):
            dve.wait_ge(root_out, n)
            link(nc.vector.reciprocal(sm[:, 2, :], sm[:, 1, :]))
            link(nc.vector.tensor_tensor(sm[:, 3, :], sm[:, 2, :], sm[:, 2, :], ALU.mult))
            link(nc.vector.tensor_tensor(sm[:, 3, :], sm[:, 3, :], sm[:, 0, :], ALU.mult))
            link(nc.vector.tensor_scalar(sm[:, 3, :], sm[:, 3, :], -0.5, 1.5, ALU.mult, ALU.add))
            link(nc.vector.tensor_tensor(out_ap, sm[:, 3, :], sm[:, 2, :], ALU.mult))

        def dve_group_var(dve, link, n):
            dve.wait_ge(grp_ready, n)
            link(nc.vector.tensor_copy(gm[:, :, :].rearrange("p s c -> p (s c)"), VT[:, 0:2 * CC]))
            link(nc.vector.tensor_tensor(sm[:, 4, :], gm[:, 0, :], gm[:, 0, :], ALU.mult))
            link(nc.vector.tensor_tensor(sm[:, 5, :], gm[:, 1, :], sm[:, 4, :], ALU.subtract))
            nc.vector.tensor_scalar(sm[:, 0, :], sm[:, 5, :], EPS, None, ALU.add).then_inc(root_in, 1)

        def dve_affine(link, dst, rate, weight, bias, done):
            if weight is not None:
                link(nc.vector.tensor_tensor(dst[:, 0, :], rate, weight, ALU.mult))
            link(nc.vector.tensor_tensor(sm[:, 7, :], gm[:, 0, :], dst[:, 0, :], ALU.mult))
            if bias is None:
                nc.vector.tensor_scalar(dst[:, 1, :], sm[:, 7, :], -1.0, None, ALU.mult).then_inc(done, 1)
            else:
                nc.vector.tensor_tensor(dst[:, 1, :], bias, sm[:, 7, :], ALU.subtract).then_inc(done, 1)

        with nc.Block() as block:
            @block.sync
            def _(sp):
                loads = [(ident[:, :], ident_c), (gmean[:, :], gmean_c), (allmean[:, :], all_c),
                         (base[:, :, :], base_c), (wqkv[:, :, :], wqkvT), (wout[:, :], woutT),
                         (wc[:, :, :], wcT)]
                loads += [(vecs[:, i, :], v) for i, v in enumerate((gamma, beta, bout, bconv, gnw, gnb))]
                for dst, src in loads:
                    sp.dma_start(dst, src).then_inc(loaded, 16)
                sp.wait_ge(ones_set, 3)
                sp.dma_start(woff[:, :, 0:OFFS], woffT).then_inc(loaded, 16)
                for t in range(4):
                    sp.dma_start(v_boff[DH * t:DH * t + OFFS, :], boff).then_inc(loaded, 16)
                n = 16 * (len(loads) + 5)
                sp.wait_ge(ring_zero, 1)
                rows = LEAD + HP * WP - PTILES * P
                sp.dma_start(tab[PTILES * P:LEAD + HP * WP, :], corners[0][0:rows, :]).then_inc(stored[0], 16)
                sp.dma_start(tab[0:LEAD, :], corners[0][0:LEAD, :]).then_inc(stored[0], 16)
                sp.wait_ge(stored[0], 32)
                sp.wait_ge(loaded, n)

            @block.gpsimd
            def _(pool):
                nc.gpsimd.memset(ones[:, :], 1.0).then_inc(ones_set, 1)
                nc.gpsimd.memset(woff[:, :, :], 0.0).then_inc(ones_set, 1)
                nc.gpsimd.memset(v_boff[:, :], 0.0).then_inc(ones_set, 1)
                nc.gpsimd.memset(corners[0][:, :], 0.0).then_inc(ring_zero, 1)

            @block.vector
            def _(dve):
                dve.wait_ge(loaded, 16 * 18)
                nc.vector.tensor_copy(identh[:, :], ident[:, :]).then_inc(chain, 1)
        clear()

        def load_q(sp, n):
            cols = bass.ds(n * NC, NC)
            for r, part in enumerate((0, 0, 1)):
                sp.dma_start(qn[DH * r:DH * (r + 1), :, :],
                             qkp[0, part, :, cols].rearrange("(h c) j -> c h j", h=HEADS)).then_inc(q_loaded, 16)

        def pe_max(pe, u, MX=MX):
            t, h, j = u // (HEADS * CHUNKS), u // CHUNKS % HEADS, u % CHUNKS
            if u >= len(MX):
                pe.wait_ge(mx_read, u - len(MX) + 1)
            nc.tensor.matmul(MX[u % len(MX)], qn[0:3 * DH, h, t * P:(t + 1) * P], kst[0:3 * DH, h, j * NC:(j + 1) * NC],
                             start=True, stop=True).then_inc(mx_full, 1)

        def dve_max(dve, u, MX=MX):
            dve.wait_ge(mx_full, u + 1)
            nc.vector.reduce_max(mx[:, u // CHUNKS, u % CHUNKS:u % CHUNKS + 1], MX[u % len(MX)],
                                 AX.X).then_inc(mx_read, 1)

        def dve_neg(dve, link, units, per_row):
            dve.wait_ge(mx_read, units)
            link(nc.vector.reduce_max(neg[:, :], mx[:, :, 0:per_row], AX.X))
            link(nc.vector.tensor_scalar(neg[:, :], neg[:, :], -1.0 / ONE, None, ALU.mult))
            link(nc.vector.tensor_copy(negp[:, :, 0], neg[:, :]))
            link(nc.vector.tensor_tensor(neg2[:, :], neg[:, :], negp[:, :, 0], ALU.subtract))
            link(nc.vector.tensor_copy(negp[:, :, 1], neg2[:, :]))
            nc.vector.tensor_tensor(negp[:, :, 2], neg2[:, :], negp[:, :, 1], ALU.subtract).then_inc(neg_ready, 1)

        def pe_neg(pe, h, units):
            if h == 0:
                pe.wait_ge(neg_ready, 1)
            if h >= 2:
                pe.wait_ge(mx_read, units + h - 1)
            for t in range(CT):
                ins = nc.tensor.matmul(MX[h % 2][3 * DH:ROWS, t * P:(t + 1) * P], negp[:, t * HEADS + h, :],
                                       identh[:, :], start=True, stop=True, tile_position=(0, 3 * DH))
            ins.then_inc(mx_full, 1)

        def dve_neg_rows(dve, h, units):
            dve.wait_ge(mx_full, units + h + 1)
            nc.vector.tensor_copy(qn[3 * DH:ROWS, h, :], MX[h % 2][3 * DH:ROWS, :]).then_inc(mx_read, 1)

        def dve_take_q(dve):
            nc.vector.tensor_copy(qc[0:ROWS, :, :], qn[0:ROWS, :, :])

        PAIRS = CHUNKS // 2
        PUNITS = CT * HEADS * PAIRS
        VUNITS = JT // 4

        def first_max(b, fb):
            with nc.Block() as block:
                @block.sync
                def _(sp):
                    if fb is not None:
                        finish_loads(sp, fb)

                @block.tensor
                def _(pe):
                    if fb is not None:
                        pe_group_means(pe, 1)

                    if b is not None:
                        for u in range(PUNITS):
                            th, j = divmod(u, PAIRS)
                            t, h = divmod(th, HEADS)
                            if u >= 3:
                                pe.wait_ge(mx_read, u - 2)
                            for i in range(2):
                                cols = slice((2 * j + i) * NC, (2 * j + i + 1) * NC)
                                ins = nc.tensor.matmul(WIDE[u % 3][:, i * NC:(i + 1) * NC],
                                                       qn[0:3 * DH, h, t * P:(t + 1) * P], kst[0:3 * DH, h, cols],
                                                       start=True, stop=True)
                            ins.then_inc(mx_full, 1)
                        for h in range(HEADS):
                            pe_neg(pe, h, PUNITS)

                @block.scalar
                def _(act):
                    if fb is not None:
                        act_root(act, 1)
                        act.wait_ge(aff_ready, 1)
                        for i in range(CHUNKS):
                            finish_act(act, i)

                @block.vector
                def _(dve):
                    link = linker(dve)
                    if fb is not None:
                        dve_moments(link, st)
                        dve_group_var(dve, link, 1)
                        dve_rsqrt(dve, link, sm[:, 6, :], 1)
                        dve_affine(link, aff, sm[:, 6, :], v_gnw, v_gnb, aff_ready)
                    if b is not None:
                        for u in range(PUNITS):
                            dve.wait_ge(mx_full, u + 1)
                            nc.vector.reduce_max(mx[:, u // PAIRS, u % PAIRS:u % PAIRS + 1], WIDE[u % 3], AX.X)\
                                .then_inc(mx_read, 1)
                            if fb is not None and u % 8 == 7:
                                finish_dve(dve, u // 8)
                        dve_neg(dve, link, PUNITS, PAIRS)
                        for h in range(HEADS):
                            dve_neg_rows(dve, h, PUNITS)
                        dve.wait_ge(mx_read, PUNITS + HEADS)
                        dve_take_q(dve)
                    else:
                        for n in range(CHUNKS):
                            finish_dve(dve, n)
            clear()

        fbufs = [t.rearrange("p (a c n) -> p a c n", a=2, c=CC) for t in pflat[0:2] + quarter[1:3]]

        def finish_loads(sp, b):
            def load(n):
                if n >= FBUFS:
                    sp.wait_ge(stored[n % FBUFS], 16 * (n // FBUFS))
                cols = slice(n * NC, (n + 1) * NC)
                sp.dma_start(fbufs[n % FBUFS][:, 0, :, :], ys[:, :, cols]).then_inc(in_loaded[n % FBUFS], 16)
                sp.dma_start(fbufs[n % FBUFS][:, 1, :, :], x1s[b, :, :, cols]).then_inc(in_loaded[n % FBUFS], 16)
            for n in range(FBUFS - 1):
                load(n)
            for n in range(CHUNKS):
                if n + FBUFS - 1 < CHUNKS:
                    load(n + FBUFS - 1)
                sp.wait_ge(out_ready[n % FBUFS], CC * (n // FBUFS + 1))
                sp.dma_start(ov[b, :, :, n * NC:(n + 1) * NC], fbufs[n % FBUFS][:, 0, :, :]).then_inc(stored[n % FBUFS], 16)
            for i in range(FBUFS):
                sp.wait_ge(stored[i], 16 * CHUNKS // FBUFS)

        def finish_act(act, n):
            act.wait_ge(in_loaded[n % FBUFS], 32 * (n // FBUFS + 1))
            for c in range(CC):
                nc.scalar.activation(fbufs[n % FBUFS][:, 1, c, :], fbufs[n % FBUFS][:, 1, c, :], ACT.Identity,
                                     bias=aff[:, 1, c:c + 1]).then_inc(norm_act, 1)

        def finish_dve(dve, n):
            dve.wait_ge(norm_act, CC * (n + 1))
            for c in range(CC):
                y = fbufs[n % FBUFS][:, 0, c, :]
                nc.vector.scalar_tensor_tensor(y, y, aff[:, 0, c:c + 1], fbufs[n % FBUFS][:, 1, c, :],
                                               ALU.mult, ALU.add).then_inc(out_ready[n % FBUFS], 1)

        def chunk(b, ic, attn, prev, nxt, conv):
            plan = max_plan(conv) if nxt else [0] * JT
            slot = SLOT_OF if conv else {}
            mx_banks = MX if conv else MX + [Y]
            s_banks = [(S + MX)[u % 4] if u < FROM * HEADS or not nxt else
                       S[u % 2] if conv else (S + [VT])[u % 3] for u in range(JT * HEADS)]

            with nc.Block() as block:
                @block.sync
                def _(sp):
                    if prev:
                        sp.dma_start(xr[:, :, :], xv[b, :, :, bass.ds(ic * NC - NC, NC)]).then_inc(loaded, 16)
                    if nxt:
                        load_q(sp, ic + 1)
                    if not attn and not conv:
                        for c in range(CC):
                            sp.dma_start(xs[:, c, 0:N - NC], x1s[b, :, c, 0:N - NC]).then_inc(x_loaded, 16)
                    if prev:
                        sp.wait_ge(x1_ready, CC)
                        sp.dma_start(x1s[b, :, :, bass.ds(ic * NC - NC, NC)], xr[:, :, :]).then_inc(stored[0], 16)
                    if conv:
                        for s in range(SUBS):
                            sp.wait_ge(y_ready, CC * (s + 1))
                            sp.dma_start(ys[:, :, bass.ds(ic * NC + s * ST * P, ST * P)], yc[s][:, :, :])\
                                .then_inc(stored[1], 16)
                    if prev:
                        sp.wait_ge(stored[0], 16)
                    if not attn and not conv:
                        sp.wait_ge(x_loaded, 16 * CC)
                    if nxt:
                        sp.wait_ge(q_loaded, 16 * 3)
                    if conv:
                        sp.wait_ge(stored[1], 16 * SUBS)

                @block.gpsimd
                def _(pool):
                    if conv:
                        nc.gpsimd.tensor_copy(idxc[:, :], widx[:, :, :].rearrange("p t k -> p (t k)")
                                              [:, bass.ds(ic * CT * TAPS, CT * TAPS)]).then_inc(idx_ready, 1)
                        pool.wait_ge(idx_ready, 1)

                    def gather(s):
                        for i in range(ST):
                            u = s * ST + i
                            col = (s // TAPS * ST + i) * TAPS + s % TAPS
                            if u >= NCORN:
                                pool.wait_ge(blended, u - NCORN + 1)
                            nc.gpsimd.indirect_dma_start(
                                corners[u % NCORN][:, :], None, tab,
                                bass.IndirectOffsetOnAxis(ap=idxc[:, col:col + 1].bitcast(U32), axis=0))\
                                .then_inc(gathered[u % NCORN], 16)
                    ahead = NCORN // ST
                    if conv:
                        for s in range(ahead):
                            gather(s)
                    for jt in range(JT):
                        g, r = divmod(jt, SUMG)
                        if attn and r and jt < JT - SUMG:
                            n = g * (SUMG - 1) + r - 1
                            pool.wait_ge(exp_done, HEADS * (jt + 1))
                            if r == 1 and g >= 2:
                                pool.wait_ge(sum_used, g - 1)
                            if r > 1:
                                pool.wait_ge(p_added, n)
                            left = probs[(jt - 1) % RING] if r == 1 else psums[g % 2]
                            nc.gpsimd.tensor_tensor(psums[g % 2], left, probs[jt % RING], ALU.add).then_inc(p_added, 1)
                        v = slot.get(jt)
                        if v is not None and v + ahead < STEPS:
                            gather(v + ahead)
                    if conv:
                        for i in range(NCORN):
                            pool.wait_ge(gathered[i], 16 * (ST * STEPS // NCORN))

                @block.scalar
                def _(act):
                    if conv:
                        act.wait_ge(w_ready, 1)

                    def first(s):
                        if s >= 3:
                            act.wait_ge(vt_full, s - 2)
                        for i in range(ST):
                            u = s * ST + i
                            col = (s // TAPS * ST + i) * TAPS + s % TAPS
                            act.wait_ge(gathered[u % NCORN], 16 * (u // NCORN + 1))
                            nc.scalar.activation(vpix[s % 3][:, i, :], corners[u % NCORN][:, 0:C], ACT.Copy,
                                                 scale=wcur[:, 0, col:col + 1]).then_inc(first_corner, 1)

                    def evacuate(s):
                        act.wait_ge(vt_full, s + 1)
                        if s >= 2:
                            act.wait_ge(conv_done, s - 1)
                        nc.scalar.activation(vT[s % 2][:, :, :].rearrange("p c n -> p (c n)"), VT,
                                             ACT.Copy).then_inc(vt_sb, 1)

                    def finish(sub):
                        act.wait_ge(conv_done, TAPS * (sub + 1))
                        for o in range(CC):
                            nc.scalar.activation(yc[sub][:, o, :], Y[:, o * ST * P:(o + 1) * ST * P], ACT.Identity,
                                                 bias=v_bconv[:, o:o + 1]).then_inc(y_ready, 1)
                    for jt in range(JT):
                        v = slot.get(jt)
                        for h in range(HEADS):
                            if attn:
                                u = jt * HEADS + h
                                if h == 0 and jt >= RING:
                                    g, r = divmod(jt - RING, SUMG)
                                    act.wait_ge(p_used, jt - RING + 1)
                                    if g < JT // SUMG - 1:
                                        act.wait_ge(p_added, g * (SUMG - 1) + max(1, r))
                                act.wait_ge(s_full, u + 1)
                                nc.scalar.activation(probs[jt % RING][:, h, :], s_banks[u], ACT.Exp,
                                                     scale=escale[:, :]).then_inc(exp_done, 1)
                            if h == 1 and v is not None:
                                if v == 0:
                                    first(0)
                                if v + 1 < STEPS:
                                    first(v + 1)
                        if v is not None:
                            if 1 <= v <= STEPS:
                                evacuate(v - 1)
                            if v == TAPS + 1:
                                finish(0)
                        if conv and jt == NEG_AT:
                            finish(1)
                    if not attn and not conv:
                        for o in range(CC):
                            act.wait_ge(x1_ready, o + 1)
                            nc.scalar.activation(xs[:, o, N - NC:N], xr[:, o, :], ACT.Copy)
                    if attn:
                        act.wait_ge(sum_used, JT // SUMG - 1 + SUMG)
                        nc.scalar.activation(rsum[:, :], SUM, ACT.Copy).then_inc(attn_ready, 1)

                @block.vector
                def _(dve):
                    link = linker(dve)
                    if conv:
                        nc.vector.tensor_copy(wcur[:, :, :], wall[:, :, :, :].rearrange("p q t k -> p q (t k)")
                                              [:, :, bass.ds(ic * CT * TAPS, CT * TAPS)]).then_inc(w_ready, 1)
                        dve.wait_ge(w_ready, 1)
                    if prev:
                        link(nc.vector.reciprocal(rsum[:, :], rsum[:, :]))
                        nc.vector.tensor_tensor(an[:, :], an[:, :], rsum[:, :], ALU.mult).then_inc(norm_dve, 1)

                    def project():
                        dve.wait_ge(loaded, 16)
                        for o in range(CC):
                            dve.wait_ge(proj_full, o + 1)
                            nc.vector.scalar_tensor_tensor(xr[:, o, :], (VT, Y)[o], v_bout[:, o:o + 1], xr[:, o, :],
                                                           ALU.add, ALU.add).then_inc(x1_ready, 1)

                    def x1_stats():
                        for o in range(CC):
                            dve.wait_ge(x1_ready, o + 1)
                            nc.vector.bn_stats(st1[:, o, bass.ds(ic - 1, 1), :].rearrange("p a s -> p (a s)"),
                                               xr[:, o, :])

                    def y_stats(sub):
                        dve.wait_ge(y_ready, CC * (sub + 1))
                        for o in range(CC):
                            nc.vector.bn_stats(st[:, o, bass.ds(ic * SUBS + sub, 1), :].rearrange("p a s -> p (a s)"),
                                               yc[sub][:, o, :])

                    def blend(s, q):
                        for i in range(ST):
                            u = s * ST + i
                            col = (s // TAPS * ST + i) * TAPS + s % TAPS
                            v = vpix[s % 3][:, i, :]
                            if q == 1:
                                dve.wait_ge(gathered[u % NCORN], 16 * (u // NCORN + 1))
                                dve.wait_ge(first_corner, u + 1)
                            else:
                                dve.wait_ge(blend_chain, (s * 2 + q - 2) * ST + i + 1)
                            nc.vector.scalar_tensor_tensor(v, corners[u % NCORN][:, q * C:(q + 1) * C],
                                                           wcur[:, q, col:col + 1], v, ALU.mult, ALU.add)\
                                .then_inc(blended if q == 3 else blend_chain, 1)

                    unit = 0
                    for jt in range(JT):
                        v = slot.get(jt)
                        step = v if v is not None and v < STEPS else None
                        for n in range(max(plan[jt], 3)):
                            if n < plan[jt]:
                                dve_max(dve, unit, mx_banks)
                                unit += 1
                            if step is not None and n < 3:
                                blend(step, n + 1)
                        if prev and jt == FROM - 1:
                            project()
                        if prev and jt == (JT // 2 if attn else FROM):
                            x1_stats()
                        if v == TAPS + 2:
                            y_stats(0)
                        if conv and jt == NEG_AT:
                            y_stats(1)
                        if nxt and jt == NEG_AT - 1:
                            dve_neg(dve, link, MAX_UNITS, CHUNKS)
                        if nxt and jt >= NEG_AT:
                            for h in range(2 * (jt - NEG_AT), 2 * (jt - NEG_AT) + 2):
                                dve_neg_rows(dve, h, MAX_UNITS)
                    if nxt:
                        dve.wait_ge(mx_read, MAX_UNITS + HEADS)
                        dve.wait_ge(q_loaded, 16 * 3)
                        dve.wait_ge(s_full, JT * HEADS)
                        dve_take_q(dve)
                    if attn:
                        dve.wait_ge(p_used, JT)
                        nc.vector.tensor_copy(an[:, :], PV).then_inc(attn_ready, 1)

                @block.tensor
                def _(pe):
                    def turn(s):
                        pe.wait_ge(blended, ST * (s + 1))
                        if s:
                            pe.wait_ge(vt_sb, s)
                        elif prev:
                            pe.wait_ge(x1_ready, 1)
                        for c in range(CC):
                            for i in range(ST):
                                ins = nc.tensor.transpose(VT[:, (c * ST + i) * P:(c * ST + i + 1) * P],
                                                          vpix[s % 3][:, i, c * P:(c + 1) * P], ident[:, :])
                        ins.then_inc(vt_full, 1)

                    def convolve(s, c):
                        sub, tap = divmod(s, TAPS)
                        if c == 0:
                            pe.wait_ge(vt_sb, s + 1)
                            if tap == 0 and sub:
                                pe.wait_ge(y_ready, CC * sub)
                            if s == 0 and prev:
                                pe.wait_ge(x1_ready, CC)
                        for o in range(CC):
                            ins = nc.tensor.matmul(Y[:, o * ST * P:(o + 1) * ST * P],
                                                   wc[:, c * TAPS + tap, o * P:(o + 1) * P], vT[s % 2][:, c, :],
                                                   start=tap == 0 and c == 0 and o == 0,
                                                   stop=tap == TAPS - 1 and c == CC - 1, skip_group_check=True)
                        if c == CC - 1:
                            ins.then_inc(conv_done, 1)

                    def scores(jt, h):
                        u = jt * HEADS + h
                        earlier = max((n for n in range(u) if s_banks[n] is s_banks[u]), default=None)
                        if earlier is not None:
                            pe.wait_ge(exp_done, earlier + 1)
                        elif prev and u >= FROM * HEADS:
                            pe.wait_ge(x1_ready, 1)
                        nc.tensor.matmul(s_banks[u], kst[0:ROWS, h, jt * P:(jt + 1) * P], qc[0:ROWS, h, :], start=True,
                                         stop=True).then_inc(s_full, 1)

                    def sum_keys(added, start, stop):
                        for h in range(HEADS):
                            ins = nc.tensor.matmul(SUM[h * DH:(h + 1) * DH, :], ones[:, :], added[:, h, :],
                                                   start=start, stop=stop, tile_position=(0, h * DH),
                                                   skip_group_check=True)
                        ins.then_inc(sum_used, 1)

                    def weigh(jt):
                        pe.wait_ge(exp_done, HEADS * (jt + 1))
                        if jt >= JT - SUMG:
                            sum_keys(probs[jt % RING], False, jt == JT - 1)
                        for h in range(HEADS):
                            band = slice(h * DH, (h + 1) * DH)
                            ins = nc.tensor.matmul(PV[band, :], vsb[:, jt, band], probs[jt % RING][:, h, :],
                                                   start=jt == 0, stop=jt == JT - 1, tile_position=(0, h * DH),
                                                   skip_group_check=True)
                        ins.then_inc(p_used, 1)

                    def add_up(g):
                        pe.wait_ge(p_added, (SUMG - 1) * (g + 1))
                        sum_keys(psums[g % 2], g == 0, False)

                    unit = 0
                    for jt in range(JT):
                        if nxt and jt == FROM:
                            pe.wait_ge(q_loaded, 16 * 3)
                            pe.wait_ge(exp_done, FROM * HEADS)
                            if prev and not conv:
                                pe.wait_ge(x1_ready, CC)
                        units = list(range(unit, unit + plan[jt]))
                        unit += plan[jt]
                        v = slot.get(jt)

                        def maxima(m=1):
                            for _ in range(m):
                                if units:
                                    pe_max(pe, units.pop(0), mx_banks)
                        if attn:
                            scores(jt, 0)
                        maxima()
                        if v is not None and v >= 2:
                            convolve(v - 2, 0)
                        if attn:
                            scores(jt, 1)
                        maxima()
                        if attn and jt:
                            weigh(jt - 1)
                        if len(units) > 2:
                            maxima()
                        if attn:
                            scores(jt, 2)
                        maxima(1)
                        if v is not None and 1 <= v <= STEPS:
                            turn(v - 1)
                        if attn and jt > SUMG and (jt - 1) % SUMG == 0:
                            add_up((jt - 1) // SUMG - 1)
                        if attn:
                            scores(jt, 3)
                        maxima()
                        if v is not None and v >= 2:
                            convolve(v - 2, 1)
                        maxima(len(units))
                        if prev and jt == FROM - 1:
                            pe.wait_ge(norm_dve, 1)
                            for o in range(CC):
                                nc.tensor.matmul((VT, Y)[o], wout[:, o * P:(o + 1) * P], an[:, :], start=True,
                                                 stop=True).then_inc(proj_full, 1)
                        if nxt and jt >= NEG_AT:
                            for h in range(2 * (jt - NEG_AT), 2 * (jt - NEG_AT) + 2):
                                pe_neg(pe, h, MAX_UNITS)
                    if attn:
                        weigh(JT - 1)
            clear()


        def load_k(sp, h, heads):
            for r, part in enumerate((0, 1, 0)):
                sp.dma_start(kst[DH * r:DH * (r + 1), h:h + heads, :],
                             qkp[1, part, h * DH:(h + heads) * DH, :].rearrange("(h c) j -> c h j", h=heads))\
                    .then_inc(k_loaded, 16)

        PX_FIRST = 8

        def between(pb, b):
            pre = 1 if pb is not None else 0

            with nc.Block() as block:
                @block.sync
                def _(sp):
                    if pb is not None:
                        sp.wait_ge(norm_act, 1)
                        sp.wait_ge(norm_dve, 1)
                    if b is not None:
                        for c in range(CC):
                            sp.dma_start(xs[:, c, :], xv[b, :, c, :]).then_inc(x_loaded, 16)
                    if pb is not None:
                        for g, m in enumerate(PGROUPS):
                            sp.wait_ge(px_act, g + 1)
                            sp.wait_ge(px_dve, min(g + 1, PTILES // 4))
                            for q in range(4):
                                first = LEAD + 4 * g * P - (q // 2 * WP + q % 2)
                                dst = tab[first:first + m * P, q * C:(q + 1) * C].rearrange("(t p) c -> p t c", p=P)
                                src = corners[g % 4][:, 0:m * C].rearrange("p (t c) -> p t c", t=m)
                                sp.dma_start(dst, src).then_inc(px_stored[g % 4], 16)
                    if b is not None:
                        for i in range(2 * CHUNKS):
                            which, n = 1 - i // CHUNKS, i % CHUNKS
                            sp.wait_ge(qk_lo, i + 1)
                            sp.dma_start(qkp[which, :, :, n * NC:(n + 1) * NC].rearrange("r p n -> p r n"),
                                         parts[i % 4][:, :, :]).then_inc(stored[i % 4], 16)
                            if i == CHUNKS - 1:
                                for n in range(4):
                                    sp.wait_ge(stored[n], 16 * CHUNKS // 4)
                                load_k(sp, 2, 2)
                            if i == CHUNKS + CHUNKS // 2 - 1:
                                load_k(sp, 0, 1)
                        load_k(sp, 1, 1)
                        for n in range(4):
                            sp.wait_ge(stored[n], 16 * 2 * CHUNKS // 4)
                        load_q(sp, 0)
                        sp.wait_ge(k_loaded, 16 * 9)
                        sp.wait_ge(q_loaded, 16 * 3)
                        sp.wait_ge(x_loaded, 16 * CC)
                    if pb is not None:
                        for i in range(4):
                            sp.wait_ge(px_stored[i], 64 * len(PGROUPS[i::4]))

                @block.gpsimd
                def _(pool):
                    if pb is not None:
                        for c in range(CC):
                            nc.gpsimd.memset(h1[:, c, 0, :], 0.0)
                            nc.gpsimd.memset(h1[:, c, HP - 1, :], 0.0)
                            nc.gpsimd.memset(h1[:, c, 1:HP - 1, 0:1], 0.0)
                            nc.gpsimd.memset(h1[:, c, 1:HP - 1, WP - 1:WP], 0.0).then_inc(ring_zero, 1)
                    if b is not None:
                        pool.wait_ge(amax_ready, 1)
                        nc.gpsimd.partition_all_reduce(pow2[:, :], amax2[:, :], P, RMAX).then_inc(amax_all, 1)
                        for h, n, units in ((2, 2, CHUNKS), (0, 1, CHUNKS + CHUNKS // 2)):
                            pool.wait_ge(qk_lo, units)
                            nc.gpsimd.memset(kst[3 * DH:ROWS, h:h + n, :], ONE).then_inc(ones_set, 1)
                        pool.wait_ge(qk_lo, 2 * CHUNKS)
                        nc.gpsimd.memset(kst[3 * DH:ROWS, 1, 0:N // 2], ONE).then_inc(ones_set, 1)

                @block.scalar
                def _(act):
                    def act_pixels(j):
                        if j >= 8:
                            act.wait_ge(px_stored[j // 2 % 4], 64 * (j // 8))
                        act.wait_ge(px_full, j + 1)
                        nc.scalar.activation(corners[j // 2 % 4][:, 0:NC], banks[2 + j % 4], ACT.Copy).then_inc(px_act, 1)

                    if pb is not None:
                        act_root(act, 1)
                        act.wait_ge(aff_ready, 1)
                        nc.scalar.activation(h1[:, 0, 1:H + 1, 1:W + 1],
                                             xs[:, 0, :].rearrange("p (y x) -> p y x", x=W), ACT.Identity,
                                             bias=aff[:, 1, 0:1], scale=aff[:, 0, 0:1]).then_inc(norm_act, 1)
                        for j in range(0, PX_FIRST, 2):
                            act_pixels(j)
                    if b is not None:
                        act_root(act, pre + 1)
                        act_root(act, pre + 2)
                        act.wait_ge(aff_ready, pre + 1)
                        nc.scalar.activation(xs[:, 0, :], xs[:, 0, :], ACT.Identity, bias=affx[:, 1, 0:1],
                                             scale=affx[:, 0, 0:1]).then_inc(norm_act, 1)
                    if pb is not None:
                        for j in range(PX_FIRST, PTILES // 2, 2):
                            act_pixels(j)
                        for r in range(2):
                            act.wait_ge(off_full, r + 1)
                            nc.scalar.activation(pflat[0][:, r * NC:(r + 1) * NC], S[r], ACT.Identity,
                                                 bias=v_boff[:, :]).then_inc(off_sb, 1)
                    if b is not None:
                        for i in range(2 * CHUNKS):
                            which, n = 1 - i // CHUNKS, i % CHUNKS
                            act.wait_ge(qk_ps, i + 1)
                            nc.scalar.activation(qkf[:, which, n * NC:(n + 1) * NC], banks[i % 4], ACT.Copy)\
                                .then_inc(qk_sb, 1)
                        def act_values(act, i):
                            act.wait_ge(v_ps, i + 1)
                            nc.scalar.activation(vsb[:, 4 * i:4 * i + 4, :].rearrange("p j c -> p (j c)"),
                                                 VB[i % 2], ACT.Copy).then_inc(v_sb, 1)
                        act.wait_ge(lift_ready, 1)
                        for i in range(2 * CHUNKS):
                            which, n = 1 - i // CHUNKS, i % CHUNKS
                            if i >= 4:
                                act.wait_ge(stored[i % 4], 16 * (i // 4))
                            act.wait_ge(qk_sb, i + 1)
                            nc.scalar.activation(parts[i % 4][:, 0, :], qkf[:, which, n * NC:(n + 1) * NC], ACT.Copy,
                                                 scale=lift[:, which:which + 1]).then_inc(qk_hi, 1)
                            if i % 2:
                                act_values(act, i // 2)

                @block.tensor
                def _(pe):
                    def turn_pixels(j):
                        if j >= 4:
                            pe.wait_ge(px_dve if j % 2 else px_act, (j - 4) // 2 + 1)
                        for i in range(2):
                            for c in range(CC):
                                e0 = (2 * j + i) * P
                                ins = nc.tensor.transpose(banks[2 + j % 4][:, (i * CC + c) * P:(i * CC + c + 1) * P],
                                                          h1flat[:, c, e0:e0 + P], ident[:, :])
                        ins.then_inc(px_full, 1)

                    def sample_mean():
                        pe.wait_ge(mom_ready, pre + 2)
                        nc.tensor.matmul(VT[:, 4 * CC:5 * CC], allmean[:, :], sm[:, 9, :], start=True, stop=True)\
                            .then_inc(grp_ready, 1)

                    if pb is not None:
                        pe_group_means(pe, 1)
                        pe.wait_ge(norm_act, 1)
                        pe.wait_ge(norm_dve, 1)
                        pe.wait_ge(ring_zero, CC)
                        for r in range(2):
                            for c in range(CC):
                                for tap in range(TAPS):
                                    ky, kx = divmod(tap, K)
                                    for t in range(4):
                                        y0 = 8 * (4 * r + t) + ky
                                        ins = nc.tensor.matmul(
                                            S[r][DH * t:DH * (t + 1), :], woff[:, c * TAPS + tap, :],
                                            h1[:, c, y0:y0 + 8, kx:kx + W], start=c == 0 and tap == 0,
                                            stop=c == CC - 1 and tap == TAPS - 1, tile_position=(0, DH * t),
                                            skip_group_check=True)
                                    if r == 0 and c == 0 and tap < PX_FIRST:
                                        turn_pixels(tap)
                                    if r == 1 and c == 1 and PX_FIRST + tap < PTILES // 2:
                                        turn_pixels(PX_FIRST + tap)
                                if c == CC - 1:
                                    ins.then_inc(off_full, 1)
                                if b is not None and (r, c) == (0, CC - 1):
                                    pe_group_means(pe, pre + 1)
                                if b is not None and (r, c) == (1, 0):
                                    sample_mean()
                        pe.wait_ge(px_act, (PTILES // 2 + 1) // 2)
                        pe.wait_ge(px_dve, PTILES // 4)
                        for r in range(2):
                            pe.wait_ge(off_sb, r + 1)
                            for q in range(4):
                                ins = nc.tensor.transpose(MX[r][:, q * P:(q + 1) * P],
                                                          pflat[0][:, r * NC + q * P:r * NC + (q + 1) * P], ident[:, :])
                            ins.then_inc(offT_full, 1)
                    else:
                        pe_group_means(pe, pre + 1)
                        sample_mean()
                    if b is not None:
                        pe.wait_ge(norm_act, pre + 1)
                        pe.wait_ge(norm_dve, pre + 1)
                        if pb is not None:
                            pe.wait_ge(off_sb, 2)
                            pe.wait_ge(offT_read, 2)
                        for i in range(2 * CHUNKS):
                            which, n = 1 - i // CHUNKS, i % CHUNKS
                            if i >= 4:
                                pe.wait_ge(qk_sb, i - 3)
                            for c in range(CC):
                                ins = nc.tensor.matmul(banks[i % 4], wqkv[:, c, which * HID:(which + 1) * HID],
                                                       xs[:, c, n * NC:(n + 1) * NC], start=c == 0, stop=c == CC - 1)
                            ins.then_inc(qk_ps, 1)
                        for i in range(VUNITS):
                            if i >= 2:
                                pe.wait_ge(v_sb, i - 1)
                            elif i == 0:
                                pe.wait_ge(root_in, pre + 2)
                            for q in range(4):
                                j = 4 * i + q
                                for c in range(CC):
                                    ins = nc.tensor.matmul(VB[i % 2][:, q * P:(q + 1) * P],
                                                           xs[:, c, j * P:(j + 1) * P], wqkv[:, c, 2 * HID:3 * HID],
                                                           start=c == 0, stop=c == CC - 1)
                            ins.then_inc(v_ps, 1)

                @block.vector
                def _(dve):
                    link = linker(dve)

                    def dve_pixels(j):
                        if j >= 8:
                            dve.wait_ge(px_stored[j // 2 % 4], 64 * (j // 8))
                        dve.wait_ge(px_full, j + 1)
                        nc.vector.tensor_copy(corners[j // 2 % 4][:, NC:2 * NC], banks[2 + j % 4]).then_inc(px_dve, 1)

                    if pb is not None:
                        dve_moments(link, st1)
                        dve_group_var(dve, link, 1)
                        dve_rsqrt(dve, link, aff[:, 0, :], 1)
                        dve_affine(link, aff, None, None, None, aff_ready)
                        dve.wait_ge(aff_ready, 1)
                        nc.vector.tensor_scalar(h1[:, 1, 1:H + 1, 1:W + 1],
                                                xs[:, 1, :].rearrange("p (y x) -> p y x", x=W),
                                                aff[:, 0, 1:2], aff[:, 1, 1:2], ALU.mult, ALU.add).then_inc(norm_dve, 1)
                        for j in range(1, PX_FIRST, 2):
                            dve_pixels(j)
                    if b is not None:
                        dve.wait_ge(x_loaded, 16 * CC)
                        for c in range(CC):
                            for n in range(CHUNKS):
                                ins = nc.vector.bn_stats(st1[:, c, n, :], xs[:, c, n * NC:(n + 1) * NC])
                        link(ins)
                        dve_moments(link, st1)
                        dve_group_var(dve, link, pre + 1)
                        dve_rsqrt(dve, link, sm[:, 6, :], pre + 1)
                        link(nc.vector.tensor_tensor(sm[:, 8, :], sm[:, 6, :], sm[:, 6, :], ALU.mult))
                        nc.vector.tensor_tensor(sm[:, 9, :], sm[:, 8, :], sm[:, 5, :], ALU.mult).then_inc(mom_ready, 1)
                        dve.wait_ge(grp_ready, pre + 2)
                        link(nc.vector.reduce_sum(sm[:, 10, 0:1], VT[:, 4 * CC:5 * CC], AX.X))
                        link(nc.vector.tensor_scalar(sm[:, 0, 0:1], sm[:, 10, 0:1], EPS, None, ALU.add))
                        nc.vector.tensor_copy(sm[:, 0, 1:2], sm[:, 0, 0:1]).then_inc(root_in, 1)
                        dve_rsqrt(dve, link, sm[:, 8, :], pre + 2)
                        link(nc.vector.tensor_tensor(sm[:, 9, :], sm[:, 6, :], sm[:, 8, :], ALU.mult))
                        dve_affine(link, affx, sm[:, 9, :], v_gamma, v_beta, aff_ready)
                        dve.wait_ge(aff_ready, pre + 1)
                        nc.vector.tensor_scalar(xs[:, 1, :], xs[:, 1, :], affx[:, 0, 1:2], affx[:, 1, 1:2],
                                                ALU.mult, ALU.add).then_inc(norm_dve, 1)
                    if pb is not None:
                        for j in range(PX_FIRST + 1, PTILES // 2, 2):
                            dve_pixels(j)
                        for r in range(2):
                            dve.wait_ge(offT_full, r + 1)
                            nc.vector.tensor_copy(
                                offall[:, 16 * r:16 * (r + 1), :].rearrange("p (t q) o -> p q t o", t=4),
                                MX[r].rearrange("p (q t o) -> p q t o", q=4, t=4)[:, :, :, 0:OFFS])\
                                .then_inc(offT_read, 1)
                        dve.wait_ge(offT_read, 2)
                        sample_points(link)
                    if b is not None:
                        for i in range(2 * CHUNKS):
                            which, n = 1 - i // CHUNKS, i % CHUNKS
                            dve.wait_ge(qk_sb, i + 1)
                            nc.vector.reduce_max(amax[:, which, n:n + 1], qkf[:, which, n * NC:(n + 1) * NC], AX.X,
                                                 apply_absolute_value=True).then_inc(amax_read, 1)
                        dve.wait_ge(amax_read, 2 * CHUNKS)
                        link(nc.vector.reduce_max(amax2[:, :], amax[:, :, :], AX.X))
                        nc.vector.tensor_scalar(amax2[:, :], amax2[:, :], 1e-30, None, ALU.max).then_inc(amax_ready, 1)
                        dve.wait_ge(amax_all, 1)
                        link(nc.vector.tensor_scalar(pow2[:, :].bitcast(I32), pow2[:, :].bitcast(I32), 0x7F800000, None,
                                                     ALU.bitwise_and))
                        link(nc.vector.reciprocal(lift[:, :], pow2[:, :]))
                        nc.vector.tensor_scalar(lift[:, :], lift[:, :], LIFT, None, ALU.mult).then_inc(lift_ready, 1)
                        link(nc.vector.tensor_scalar(escale[:, :], pow2[:, 0:1], SCALE / LIFT / LIFT, None, ALU.mult))
                        link(nc.vector.tensor_tensor(escale[:, :], escale[:, :], pow2[:, 1:2], ALU.mult))
                        for i in range(2 * CHUNKS):
                            which, n = 1 - i // CHUNKS, i % CHUNKS
                            dve.wait_ge(qk_hi, i + 1)
                            nc.vector.scalar_tensor_tensor(parts[i % 4][:, 1, :], qkf[:, which, n * NC:(n + 1) * NC],
                                                           lift[:, which:which + 1], parts[i % 4][:, 0, :],
                                                           ALU.mult, ALU.subtract).then_inc(qk_lo, 1)
                        dve.wait_ge(qk_lo, 2 * CHUNKS)
                        nc.vector.memset(kst[3 * DH:ROWS, 1, N // 2:N], ONE).then_inc(ones_set, 1)
            clear()

        def sample_points(link):
            n = TILES * OFFS
            pos = offall[:, :, :].rearrange("p t o -> p (t o)")
            t0, t1, t2 = (pflat[1][:, i * n:(i + 1) * n] for i in range(3))
            link(nc.vector.tensor_tensor(pos, pos, base[:, :, :].rearrange("p t o -> p (t o)"), ALU.add))
            link(nc.vector.tensor_scalar(pos, pos, 0.0, float(HP - 1), ALU.max, ALU.min))
            whole = t0.bitcast(I32)
            link(nc.vector.tensor_copy(whole, pos))
            link(nc.vector.tensor_copy(t1, whole))
            link(nc.vector.tensor_tensor(t2, t1, pos, ALU.is_gt))
            link(nc.vector.tensor_tensor(t1, t1, t2, ALU.subtract))
            link(nc.vector.tensor_tensor(pos, pos, t1, ALU.subtract))
            link(nc.vector.tensor_scalar(t2, pos, -1.0, 1.0, ALU.mult, ALU.add))
            fy, fx = offall[:, :, 0:TAPS], offall[:, :, TAPS:OFFS]
            far = t2.rearrange("p (t o) -> p t o", o=OFFS)
            gy, gx = far[:, :, 0:TAPS], far[:, :, TAPS:OFFS]
            low = t1.rearrange("p (t o) -> p t o", o=OFFS)
            for q, (wy, wx) in enumerate(((gy, gx), (gy, fx), (fy, gx), (fy, fx))):
                nc.vector.tensor_tensor(wall[:, q, :, :], wy, wx, ALU.mult)
            t0v = t0.rearrange("p (t o) -> p t o", o=OFFS)[:, :, 0:TAPS]
            link(nc.vector.scalar_tensor_tensor(t0v, low[:, :, 0:TAPS], float(WP), low[:, :, TAPS:OFFS],
                                                ALU.mult, ALU.add))
            link(nc.vector.tensor_scalar(t0v, t0v, float(LEAD), None, ALU.add))
            link(nc.vector.tensor_copy(widx[:, :, :], t0v))

        def attend(b, conv):
            chunk(b, 0, True, False, True, conv)
            with nc.Fori(1, CHUNKS - 1) as ic:
                chunk(b, ic, True, True, True, conv)
            chunk(b, CHUNKS - 1, True, True, False, conv)
            chunk(b, CHUNKS, False, True, False, False)

        between(None, 0)
        first_max(0, None)
        attend(0, False)
        between(0, 1)
        first_max(1, None)
        attend(1, True)
        with nc.Fori(2, B) as b:
            between(b - 1, b)
            first_max(b, b - 2)
            attend(b, True)
        between(B - 1, None)
        first_max(None, B - 2)
        with nc.Fori(0, CHUNKS) as ic:
            chunk(None, ic, False, False, False, True)
        first_max(None, B - 1)


def kernel(**inputs):
    import numpy as _np
    import concourse.bacc as _bacc
    from concourse import mybir as _mybir
    from concourse.bass_utils import run_bass_kernel_spmd as _run

    a = {k: _np.asarray(v) for k, v in inputs.items()}

    def halves(v):
        return v.reshape(CC, P).T

    px = _np.arange(N).reshape(TILES, P)
    base = _np.zeros((P, TILES, OFFS), _np.float32)
    for k in range(TAPS):
        base[:, :, k] = (px // W + k // K).T
        base[:, :, TAPS + k] = (px % W + k % K).T
    arrays = {
        "x": a["x"],
        "gamma": halves(a["L0_conv_gamma"]),
        "beta": halves(a["L0_conv_beta"]),
        "wqkvT": a["L0_conv_w_qkv"].T.reshape(CC, P, 3 * HID).transpose(1, 0, 2),
        "woutT": a["L0_conv_w_out"].T,
        "bout": halves(a["L0_conv_b_out"]),
        "woffT": a["L1_conv_w_off"].reshape(OFFS, CC, P, TAPS).transpose(2, 1, 3, 0).reshape(P, CC * TAPS, OFFS),
        "boff": a["L1_conv_b_off"].reshape(OFFS, 1),
        "wcT": a["L1_conv_w"].reshape(C, CC, P, TAPS).transpose(2, 1, 3, 0).reshape(P, CC * TAPS, C),
        "bconv": halves(a["L1_conv_b"]),
        "gnw": halves(a["L1_conv_gn_w"]),
        "gnb": halves(a["L1_conv_gn_b"]),
        "ident": _np.eye(P, dtype=_np.float32),
        "gmean": (_np.kron(_np.eye(P // GROUP), _np.ones((GROUP, GROUP))) / GROUP).astype(_np.float32),
        "allmean": _np.full((P, P), 1.0 / C, _np.float32),
        "base": base,
    }
    arrays = {k: _np.ascontiguousarray(v) for k, v in arrays.items()}
    nc = _bacc.Bacc("TRN2", target_bir_lowering=False, num_devices=1)
    args = [nc.dram_tensor(f"in_{k}", v.shape, _mybir.dt.float32, kind="ExternalInput").ap() for k, v in arrays.items()]
    out = nc.dram_tensor("out_0", (B, C, H, W), _mybir.dt.float32, kind="ExternalOutput").ap()
    build(nc, *args, out)
    r = _run(nc, [{f"in_{k}": v for k, v in arrays.items()}], core_ids=[0])
    return r.results[0]["out_0"]
```
